# Optimizing a Trainium2 kernel written in Bass

```python
import numpy as np
import jax
import jax.numpy as jnp

def _softmax(x, axis=-1):
    return jax.nn.softmax(x, axis=axis)

def _gelu(x):
    return jax.nn.gelu(x, approximate=True)

def _silu(x):
    return jax.nn.silu(x)

def _sigmoid(x):
    return jax.nn.sigmoid(x)

def _layernorm(x, axis=-1, eps=1e-05):
    m = jnp.mean(x, axis=axis, keepdims=True)
    v = jnp.var(x, axis=axis, keepdims=True)
    return (x - m) / jnp.sqrt(v + eps)

def _scatter_add(tgt, idx, src, axis=0):
    return tgt.at[idx].add(src)

def _segment_sum(src, seg, n):
    return jax.ops.segment_sum(src, seg, n)
kernel_name = 'mk_gps_d2_gnn_r16_bc2eec'

def setup_inputs(seed: int=0):
    np.random.seed(seed)
    _w = jnp.asarray

    def _rec_inputs():
        import jax
        import jax.numpy as jnp
        _gk = jax.random.key(seed)
        x = -0.0002117 + 1 * jax.random.normal(jax.random.fold_in(_gk, 1), (3125, 256), jnp.float32)
        src = jax.random.randint(jax.random.fold_in(_gk, 2), (50000,), 0, 3125, jnp.int32)
        dst = jnp.minimum((3125 * jax.random.uniform(jax.random.fold_in(_gk, 3), (50000,)) ** 2.0).astype(jnp.int32), 49999)
        _o = jnp.argsort(dst, stable=True)
        src = src[_o]
        dst = dst[_o]
        edge_attr_2 = jax.random.uniform(jax.random.fold_in(_gk, 11), (50000, 2), jnp.float32, 0.0, 1)
        return (x, src, dst, edge_attr_2)
    x, src, dst, edge_attr_2 = _rec_inputs()

    def _L0_gnn_setup():
        import jax, jax.numpy as jnp
        import numpy as np
        N_NODES = 6250
        N_EDGES = 100000
        IN_FEATS = 256
        OUT_FEATS = 64
        NUM_HEADS = 4
        key = jax.random.key(seed)
        k_h, k_adj, k_dir, k_wf, k_wr, k_af = jax.random.split(key, 6)
        h = jax.random.normal(k_h, (N_NODES, IN_FEATS), dtype=jnp.float32)
        adj = jax.random.randint(k_adj, (2, N_EDGES), 0, N_NODES, dtype=jnp.int64)
        bit = jax.random.randint(k_dir, (N_EDGES,), 0, 2).astype(jnp.float32)
        direction = jnp.stack([bit, 1.0 - bit], axis=1)
        s_w = float(np.sqrt(6.0 / (IN_FEATS + OUT_FEATS)))
        s_a = float(np.sqrt(6.0 / (NUM_HEADS + OUT_FEATS)))
        W_forward = jax.random.uniform(k_wf, (OUT_FEATS, IN_FEATS), jnp.float32, -s_w, s_w)
        W_reverse = jax.random.uniform(k_wr, (OUT_FEATS, IN_FEATS), jnp.float32, -s_w, s_w)
        attn_forward = jax.random.uniform(k_af, (1, NUM_HEADS, OUT_FEATS), jnp.float32, -s_a, s_a)
        return {'h': h, 'adj': adj, 'direction': direction, 'W_forward': W_forward, 'W_reverse': W_reverse, 'attn_forward': attn_forward}
    _L0_gnn_all = _L0_gnn_setup()
    _L0_gnn_in = {k: v for k, v in _L0_gnn_all.items() if k in ('W_forward', 'W_reverse', 'attn_forward')}
    del _L0_gnn_all

    def _L0_mix_setup():
        import jax, jax.numpy as jnp
        import numpy as np
        EMB, HEADS, DEPTH, SEQ, BATCH = (256, 8, 4, 512, 4)
        DH = EMB // HEADS
        FF = 4 * EMB
        EPS = 1e-05

        def _layernorm(x, g, b):
            mu = x.mean(-1, keepdims=True)
            var = ((x - mu) ** 2).mean(-1, keepdims=True)
            return (x - mu) * jax.lax.rsqrt(var + EPS) * g + b

        def _linear_attn(x, Wq, Wk, Wv, Wo, bo):
            b, n, dm = x.shape
            split = lambda t: t.reshape(b, n, HEADS, DH).transpose(0, 2, 1, 3)
            scale = DH ** (-0.25)
            q = jax.nn.softmax(split(x @ Wq) * scale, axis=-1)
            k = jax.nn.softmax(split(x @ Wk) * scale, axis=-2)
            v = split(x @ Wv)
            context = jnp.einsum('bhnd,bhne->bhde', k, v)
            out = jnp.einsum('bhnd,bhde->bhne', q, context)
            out = out.transpose(0, 2, 1, 3).reshape(b, n, dm)
            return out @ Wo + bo

        def _forward(x, Wq, Wk, Wv, Wo, bo, ln1_g, ln1_b, W1, b1, W2, b2, ln2_g, ln2_b):
            for i in range(DEPTH):
                h = _layernorm(x, ln1_g[i], ln1_b[i])
                x = x + _linear_attn(h, Wq[i], Wk[i], Wv[i], Wo[i], bo[i])
                h = _layernorm(x, ln2_g[i], ln2_b[i])
                x = x + (jax.nn.gelu(h @ W1[i] + b1[i], approximate=False) @ W2[i] + b2[i])
            return x
        key = jax.random.key(seed)
        ks = jax.random.split(key, 8)
        w = lambda k, shape: jax.random.normal(k, shape, dtype=jnp.float32) * 0.02
        D = DEPTH
        return {'x': jax.random.normal(ks[0], (BATCH, SEQ, EMB), dtype=jnp.float32), 'Wq': w(ks[1], (D, EMB, EMB)), 'Wk': w(ks[2], (D, EMB, EMB)), 'Wv': w(ks[3], (D, EMB, EMB)), 'Wo': w(ks[4], (D, EMB, EMB)), 'bo': jnp.zeros((D, EMB), jnp.float32), 'ln1_g': jnp.ones((D, EMB), jnp.float32), 'ln1_b': jnp.zeros((D, EMB), jnp.float32), 'W1': w(ks[5], (D, EMB, FF)), 'b1': jnp.zeros((D, FF), jnp.float32), 'W2': w(ks[6], (D, FF, EMB)), 'b2': jnp.zeros((D, EMB), jnp.float32), 'ln2_g': jnp.ones((D, EMB), jnp.float32), 'ln2_b': jnp.zeros((D, EMB), jnp.float32)}
    _L0_mix_all = _L0_mix_setup()
    _L0_mix_in = {k: v for k, v in _L0_mix_all.items() if k in ('Wq', 'Wk', 'Wv', 'Wo', 'bo', 'ln1_g', 'ln1_b', 'W1', 'b1', 'W2', 'b2', 'ln2_g', 'ln2_b')}
    del _L0_mix_all

    def _L0_ffn_setup():
        import jax, jax.numpy as jnp
        import numpy as np
        B, T, D, H, E = (16, 256, 256, 512, 8)
        key = jax.random.key(seed)
        ks = jax.random.split(key, 5)
        x = jax.random.normal(ks[0], (B, T, D), dtype=jnp.float32)
        gate_w = jax.random.normal(ks[1], (D, E), dtype=jnp.float32) * 0.02
        gate_b = jnp.zeros((E,), dtype=jnp.float32)
        W1 = jax.random.normal(ks[2], (E, D, H), dtype=jnp.float32) * 0.02
        b1 = jnp.zeros((E, H), dtype=jnp.float32)
        W2 = jax.random.normal(ks[3], (E, H, D), dtype=jnp.float32) * 0.02
        b2 = jnp.zeros((E, D), dtype=jnp.float32)
        return {'x': x, 'gate_w': gate_w, 'gate_b': gate_b, 'W1': W1, 'b1': b1, 'W2': W2, 'b2': b2}
    _L0_ffn_all = _L0_ffn_setup()
    _L0_ffn_in = {k: v for k, v in _L0_ffn_all.items() if k in ('gate_w', 'gate_b', 'W1', 'b1', 'W2', 'b2')}
    del _L0_ffn_all

    def _L1_gnn_setup():
        import jax, jax.numpy as jnp
        import numpy as np
        N_NODES = 625
        N_EDGES = 20000
        D_IN = 256
        D_OUT = 256
        key = jax.random.key(seed)
        k1, k2, k3, k4 = jax.random.split(key, 4)
        x = jax.random.normal(k1, (N_NODES, D_IN), dtype=jnp.float32)
        edge_index = jax.random.randint(k2, (2, N_EDGES), 0, N_NODES, dtype=jnp.int64)
        weight = jax.random.normal(k3, (2 * D_IN, D_OUT), dtype=jnp.float32) / np.sqrt(2 * D_IN)
        bias = jax.random.normal(k4, (D_OUT,), dtype=jnp.float32)
        return {'x': x, 'edge_index': edge_index, 'weight': weight, 'bias': bias}
    _L1_gnn_all = _L1_gnn_setup()
    _L1_gnn_in = {k: v for k, v in _L1_gnn_all.items() if k in ('weight', 'bias')}
    del _L1_gnn_all

    def _L1_mix_setup():
        import jax, jax.numpy as jnp
        import numpy as np
        MIDC = 256
        HEADS = 8
        HEADC = MIDC // HEADS
        EPS = 1e-05

        def _ln(x, gamma, beta):
            mu = jnp.mean(x, axis=-1, keepdims=True)
            var = jnp.var(x, axis=-1, keepdims=True)
            return (x - mu) * jax.lax.rsqrt(var + EPS) * gamma + beta
        key = jax.random.key(seed)
        ks = jax.random.split(key, 8)
        B, HW, C = (8, 256, MIDC)
        s = 1.0 / np.sqrt(C)
        return {'x': jax.random.normal(ks[0], (B, HW, C), jnp.float32), 'w_qkv': jax.random.normal(ks[1], (C, 3 * C), jnp.float32) * s, 'b_qkv': jnp.zeros((3 * C,), jnp.float32), 'kln_g': jnp.ones((HEADC,), jnp.float32), 'kln_b': jnp.zeros((HEADC,), jnp.float32), 'vln_g': jnp.ones((HEADC,), jnp.float32), 'vln_b': jnp.zeros((HEADC,), jnp.float32), 'w1': jax.random.normal(ks[2], (C, C), jnp.float32) * s, 'b1': jnp.zeros((C,), jnp.float32), 'w2': jax.random.normal(ks[3], (C, C), jnp.float32) * s, 'b2': jnp.zeros((C,), jnp.float32)}
    _L1_mix_all = _L1_mix_setup()
    _L1_mix_in = {k: v for k, v in _L1_mix_all.items() if k in ('w_qkv', 'b_qkv', 'kln_g', 'kln_b', 'vln_g', 'vln_b', 'w1', 'b1', 'w2', 'b2')}
    del _L1_mix_all

    def _L1_ffn_setup():
        import jax, jax.numpy as jnp
        import numpy as np
        BN_EPS = 0.001

        def _bn(h, g, b, m, v):
            return g * (h - m) * jax.lax.rsqrt(v + BN_EPS) + b
        key = jax.random.key(seed)
        ks = jax.random.split(key, 8)
        B, F, Df = (256, 64, 256)
        E, H, D = (8, 256, 256)
        s1 = 1.0 / np.sqrt(Df)
        s2 = 1.0 / np.sqrt(H)
        return {'x': jax.random.normal(ks[0], (B, F, Df), jnp.float32), 'Wr': jax.random.normal(ks[1], (Df, E), jnp.float32) * s1, 'br': jnp.zeros((E,), jnp.float32), 'W1': jax.random.normal(ks[2], (E, Df, H), jnp.float32) * s1, 'b1': jnp.zeros((E, H), jnp.float32), 'g1': jnp.ones((E, H), jnp.float32), 'be1': jnp.zeros((E, H), jnp.float32), 'm1': jnp.zeros((E, H), jnp.float32), 'v1': jnp.ones((E, H), jnp.float32), 'W2': jax.random.normal(ks[3], (E, H, H), jnp.float32) * s2, 'b2': jnp.zeros((E, H), jnp.float32), 'g2': jnp.ones((E, H), jnp.float32), 'be2': jnp.zeros((E, H), jnp.float32), 'm2': jnp.zeros((E, H), jnp.float32), 'v2': jnp.ones((E, H), jnp.float32), 'Wo': jax.random.normal(ks[4], (E, H, D), jnp.float32) * s2, 'bo': jnp.zeros((E, D), jnp.float32)}
    _L1_ffn_all = _L1_ffn_setup()
    _L1_ffn_in = {k: v for k, v in _L1_ffn_all.items() if k in ('Wr', 'br', 'W1', 'b1', 'g1', 'be1', 'm1', 'v1', 'W2', 'b2', 'g2', 'be2', 'm2', 'v2', 'Wo', 'bo')}
    del _L1_ffn_all
    return {'x': x, 'src': src, 'dst': dst, 'edge_attr_2': edge_attr_2, 'L0_gnn_W_forward': _L0_gnn_in['W_forward'], 'L0_gnn_W_reverse': _L0_gnn_in['W_reverse'], 'L0_gnn_attn_forward': _L0_gnn_in['attn_forward'], 'L0_mix_Wq': _L0_mix_in['Wq'], 'L0_mix_Wk': _L0_mix_in['Wk'], 'L0_mix_Wv': _L0_mix_in['Wv'], 'L0_mix_Wo': _L0_mix_in['Wo'], 'L0_mix_bo': _L0_mix_in['bo'], 'L0_mix_ln1_g': _L0_mix_in['ln1_g'], 'L0_mix_ln1_b': _L0_mix_in['ln1_b'], 'L0_mix_W1': _L0_mix_in['W1'], 'L0_mix_b1': _L0_mix_in['b1'], 'L0_mix_W2': _L0_mix_in['W2'], 'L0_mix_b2': _L0_mix_in['b2'], 'L0_mix_ln2_g': _L0_mix_in['ln2_g'], 'L0_mix_ln2_b': _L0_mix_in['ln2_b'], 'L0_ffn_gate_w': _L0_ffn_in['gate_w'], 'L0_ffn_gate_b': _L0_ffn_in['gate_b'], 'L0_ffn_W1': _L0_ffn_in['W1'], 'L0_ffn_b1': _L0_ffn_in['b1'], 'L0_ffn_W2': _L0_ffn_in['W2'], 'L0_ffn_b2': _L0_ffn_in['b2'], 'L1_gnn_weight': _L1_gnn_in['weight'], 'L1_gnn_bias': _L1_gnn_in['bias'], 'L1_mix_w_qkv': _L1_mix_in['w_qkv'], 'L1_mix_b_qkv': _L1_mix_in['b_qkv'], 'L1_mix_kln_g': _L1_mix_in['kln_g'], 'L1_mix_kln_b': _L1_mix_in['kln_b'], 'L1_mix_vln_g': _L1_mix_in['vln_g'], 'L1_mix_vln_b': _L1_mix_in['vln_b'], 'L1_mix_w1': _L1_mix_in['w1'], 'L1_mix_b1': _L1_mix_in['b1'], 'L1_mix_w2': _L1_mix_in['w2'], 'L1_mix_b2': _L1_mix_in['b2'], 'L1_ffn_Wr': _L1_ffn_in['Wr'], 'L1_ffn_br': _L1_ffn_in['br'], 'L1_ffn_W1': _L1_ffn_in['W1'], 'L1_ffn_b1': _L1_ffn_in['b1'], 'L1_ffn_g1': _L1_ffn_in['g1'], 'L1_ffn_be1': _L1_ffn_in['be1'], 'L1_ffn_m1': _L1_ffn_in['m1'], 'L1_ffn_v1': _L1_ffn_in['v1'], 'L1_ffn_W2': _L1_ffn_in['W2'], 'L1_ffn_b2': _L1_ffn_in['b2'], 'L1_ffn_g2': _L1_ffn_in['g2'], 'L1_ffn_be2': _L1_ffn_in['be2'], 'L1_ffn_m2': _L1_ffn_in['m2'], 'L1_ffn_v2': _L1_ffn_in['v2'], 'L1_ffn_Wo': _L1_ffn_in['Wo'], 'L1_ffn_bo': _L1_ffn_in['bo']}

def reference(x, src, dst, edge_attr_2, L0_gnn_W_forward, L0_gnn_W_reverse, L0_gnn_attn_forward, L0_mix_Wq, L0_mix_Wk, L0_mix_Wv, L0_mix_Wo, L0_mix_bo, L0_mix_ln1_g, L0_mix_ln1_b, L0_mix_W1, L0_mix_b1, L0_mix_W2, L0_mix_b2, L0_mix_ln2_g, L0_mix_ln2_b, L0_ffn_gate_w, L0_ffn_gate_b, L0_ffn_W1, L0_ffn_b1, L0_ffn_W2, L0_ffn_b2, L1_gnn_weight, L1_gnn_bias, L1_mix_w_qkv, L1_mix_b_qkv, L1_mix_kln_g, L1_mix_kln_b, L1_mix_vln_g, L1_mix_vln_b, L1_mix_w1, L1_mix_b1, L1_mix_w2, L1_mix_b2, L1_ffn_Wr, L1_ffn_br, L1_ffn_W1, L1_ffn_b1, L1_ffn_g1, L1_ffn_be1, L1_ffn_m1, L1_ffn_v1, L1_ffn_W2, L1_ffn_b2, L1_ffn_g2, L1_ffn_be2, L1_ffn_m2, L1_ffn_v2, L1_ffn_Wo, L1_ffn_bo):
    import jax
    import jax.numpy as jnp

    def _L0_gnn_ref(h, adj, direction, W_forward, W_reverse, attn_forward):
        import jax, jax.numpy as jnp
        import numpy as np
        N_NODES = 6250
        N_EDGES = 100000
        IN_FEATS = 256
        OUT_FEATS = 64
        NUM_HEADS = 4
        N = h.shape[0]
        H = attn_forward.shape[1]
        h_fwd = h @ W_forward.T
        h_rev = h @ W_reverse.T
        src, dst = (adj[0], adj[1])
        messages = h_fwd[src] * direction[:, 0:1] + h_rev[src] * direction[:, 1:2]
        scores = jnp.einsum('ef,hf->eh', messages, attn_forward[0])
        scores = jax.nn.leaky_relu(scores, negative_slope=0.2)
        exp_scores = jnp.exp(scores - scores.max(axis=0, keepdims=True))
        sum_exp = jax.ops.segment_sum(exp_scores, dst, num_segments=N)
        norm = exp_scores / (sum_exp[dst] + 1e-10)
        outs = [jax.ops.segment_sum(messages * norm[:, hd:hd + 1], dst, num_segments=N) for hd in range(H)]
        out = jnp.stack(outs, axis=1)
        return out.reshape(N, -1)

    def _L0_mix_ref(x, Wq, Wk, Wv, Wo, bo, ln1_g, ln1_b, W1, b1, W2, b2, ln2_g, ln2_b):
        import jax, jax.numpy as jnp
        import numpy as np
        EMB, HEADS, DEPTH, SEQ, BATCH = (256, 8, 4, 512, 4)
        DH = EMB // HEADS
        FF = 4 * EMB
        EPS = 1e-05

        def _layernorm(x, g, b):
            mu = x.mean(-1, keepdims=True)
            var = ((x - mu) ** 2).mean(-1, keepdims=True)
            return (x - mu) * jax.lax.rsqrt(var + EPS) * g + b

        def _linear_attn(x, Wq, Wk, Wv, Wo, bo):
            b, n, dm = x.shape
            split = lambda t: t.reshape(b, n, HEADS, DH).transpose(0, 2, 1, 3)
            scale = DH ** (-0.25)
            q = jax.nn.softmax(split(x @ Wq) * scale, axis=-1)
            k = jax.nn.softmax(split(x @ Wk) * scale, axis=-2)
            v = split(x @ Wv)
            context = jnp.einsum('bhnd,bhne->bhde', k, v)
            out = jnp.einsum('bhnd,bhde->bhne', q, context)
            out = out.transpose(0, 2, 1, 3).reshape(b, n, dm)
            return out @ Wo + bo

        def _forward(x, Wq, Wk, Wv, Wo, bo, ln1_g, ln1_b, W1, b1, W2, b2, ln2_g, ln2_b):
            for i in range(DEPTH):
                h = _layernorm(x, ln1_g[i], ln1_b[i])
                x = x + _linear_attn(h, Wq[i], Wk[i], Wv[i], Wo[i], bo[i])
                h = _layernorm(x, ln2_g[i], ln2_b[i])
                x = x + (jax.nn.gelu(h @ W1[i] + b1[i], approximate=False) @ W2[i] + b2[i])
            return x
        return _forward(x, Wq, Wk, Wv, Wo, bo, ln1_g, ln1_b, W1, b1, W2, b2, ln2_g, ln2_b)

    def _L0_ffn_ref(x, gate_w, gate_b, W1, b1, W2, b2):
        import jax, jax.numpy as jnp
        import numpy as np
        B, T, D, H, E = (16, 256, 256, 512, 8)
        Bb, Tt, Dd = x.shape
        Ee = gate_w.shape[1]
        xf = x.reshape(-1, Dd)
        N = xf.shape[0]
        logits = xf @ gate_w + gate_b
        probs = jax.nn.softmax(logits, axis=-1)
        top2_vals, top2_idx = jax.lax.top_k(probs, 2)
        cw = jnp.zeros((N, Ee), dtype=xf.dtype).at[jnp.arange(N)[:, None], top2_idx].add(top2_vals)

        def step(acc, params):
            w1, bb1, w2, bb2, we = params
            h = jax.nn.gelu(xf @ w1 + bb1, approximate=False)
            y = h @ w2 + bb2
            return (acc + we[:, None] * y, None)
        out, _ = jax.lax.scan(step, jnp.zeros_like(xf), (W1, b1, W2, b2, cw.T))
        return out.reshape(Bb, Tt, Dd)

    def _L1_gnn_ref(x, edge_index, weight, bias):
        import jax, jax.numpy as jnp
        import numpy as np
        N_NODES = 625
        N_EDGES = 20000
        D_IN = 256
        D_OUT = 256
        n = x.shape[0]
        src, dst = (edge_index[0], edge_index[1])
        summed = jax.ops.segment_sum(x[src], dst, num_segments=n)
        deg = jax.ops.segment_sum(jnp.ones_like(src, dtype=x.dtype), dst, num_segments=n)
        agg = summed / jnp.maximum(deg, 1.0)[:, None]
        out = jnp.concatenate([x, agg], axis=-1) @ weight
        out = out / jnp.linalg.norm(out, axis=-1, keepdims=True)
        return out + bias

    def _L1_mix_ref(x, w_qkv, b_qkv, kln_g, kln_b, vln_g, vln_b, w1, b1, w2, b2):
        import jax, jax.numpy as jnp
        import numpy as np
        MIDC = 256
        HEADS = 8
        HEADC = MIDC // HEADS
        EPS = 1e-05

        def _ln(x, gamma, beta):
            mu = jnp.mean(x, axis=-1, keepdims=True)
            var = jnp.var(x, axis=-1, keepdims=True)
            return (x - mu) * jax.lax.rsqrt(var + EPS) * gamma + beta
        B, HW, C = x.shape
        bias = x
        qkv = (x @ w_qkv + b_qkv).reshape(B, HW, HEADS, 3 * HEADC)
        qkv = qkv.transpose(0, 2, 1, 3)
        q, k, v = jnp.split(qkv, 3, axis=-1)
        k = _ln(k, kln_g, kln_b)
        v = _ln(v, vln_g, vln_b)
        kv = jnp.einsum('bhnd,bhne->bhde', k, v) / HW
        out = jnp.einsum('bhnd,bhde->bhne', q, kv)
        out = out.transpose(0, 2, 1, 3).reshape(B, HW, C)
        ret = out + bias
        h = jax.nn.gelu(ret @ w1 + b1, approximate=False)
        return h @ w2 + b2 + bias

    def _L1_ffn_ref(x, Wr, br, W1, b1, g1, be1, m1, v1, W2, b2, g2, be2, m2, v2, Wo, bo):
        import jax, jax.numpy as jnp
        import numpy as np
        BN_EPS = 0.001

        def _bn(h, g, b, m, v):
            return g * (h - m) * jax.lax.rsqrt(v + BN_EPS) + b
        feat = jnp.mean(x, axis=0)
        w = jax.nn.softmax(feat @ Wr + br, axis=-1)
        h = jnp.einsum('bfd,edh->bfeh', x, W1) + b1
        h = jax.nn.relu(_bn(h, g1, be1, m1, v1))
        h = jnp.einsum('bfeh,ehk->bfek', h, W2) + b2
        h = jax.nn.relu(_bn(h, g2, be2, m2, v2))
        y = jnp.einsum('bfeh,ehd->bfed', h, Wo) + bo
        return jnp.einsum('bfed,fe->bfd', y, w)
    edge_index = jnp.stack([src, dst])
    xn = _layernorm(x, axis=-1)
    x = x + _L0_gnn_ref(xn, edge_index, edge_attr_2, L0_gnn_W_forward, L0_gnn_W_reverse, L0_gnn_attn_forward) + _L0_mix_ref(xn[None], L0_mix_Wq, L0_mix_Wk, L0_mix_Wv, L0_mix_Wo, L0_mix_bo, L0_mix_ln1_g, L0_mix_ln1_b, L0_mix_W1, L0_mix_b1, L0_mix_W2, L0_mix_b2, L0_mix_ln2_g, L0_mix_ln2_b)[0]
    x = x + _L0_ffn_ref(_layernorm(x, axis=-1)[None], L0_ffn_gate_w, L0_ffn_gate_b, L0_ffn_W1, L0_ffn_b1, L0_ffn_W2, L0_ffn_b2)[0]
    xn = _layernorm(x, axis=-1)
    x = x + _L1_gnn_ref(xn, edge_index, L1_gnn_weight, L1_gnn_bias) + _L1_mix_ref(xn[None], L1_mix_w_qkv, L1_mix_b_qkv, L1_mix_kln_g, L1_mix_kln_b, L1_mix_vln_g, L1_mix_vln_b, L1_mix_w1, L1_mix_b1, L1_mix_w2, L1_mix_b2)[0]
    x = x + _L1_ffn_ref(_layernorm(x, axis=-1)[None], L1_ffn_Wr, L1_ffn_br, L1_ffn_W1, L1_ffn_b1, L1_ffn_g1, L1_ffn_be1, L1_ffn_m1, L1_ffn_v1, L1_ffn_W2, L1_ffn_b2, L1_ffn_g2, L1_ffn_be2, L1_ffn_m2, L1_ffn_v2, L1_ffn_Wo, L1_ffn_bo)[0]
    return x

_drawn_inputs = setup_inputs


def setup_inputs(seed=0):
    import zlib

    import numpy as np

    out = dict(_drawn_inputs(seed))
    spreads = {'L0_mix_bo': (0.0, 0.1),
     'L0_mix_ln1_g': (1.0, 0.6),
     'L0_mix_ln1_b': (0.0, 0.8),
     'L0_mix_b1': (0.0, 0.1),
     'L0_mix_b2': (0.0, 0.1),
     'L0_mix_ln2_g': (1.0, 0.6),
     'L0_mix_ln2_b': (0.0, 0.679),
     'L0_ffn_gate_b': (0.0, 0.8),
     'L0_ffn_b1': (0.0, 0.8),
     'L0_ffn_b2': (0.0, 0.682),
     'L1_mix_b_qkv': (0.0, 0.1),
     'L1_mix_kln_g': (1.0, 0.6),
     'L1_mix_kln_b': (0.0, 0.378),
     'L1_mix_vln_g': (1.0, 0.6),
     'L1_mix_vln_b': (0.0, 0.306),
     'L1_mix_b1': (0.0, 0.351),
     'L1_mix_b2': (0.0, 0.27),
     'L1_ffn_br': (0.0, 0.8),
     'L1_ffn_b1': (0.0, 0.8),
     'L1_ffn_g1': (1.0, 0.6),
     'L1_ffn_be1': (0.0, 0.8),
     'L1_ffn_m1': (0.0, 0.8),
     'L1_ffn_v1': (1.0, 0.6),
     'L1_ffn_b2': (0.0, 0.735),
     'L1_ffn_g2': (1.0, 0.6),
     'L1_ffn_be2': (0.0, 0.8),
     'L1_ffn_m2': (0.0, 0.732),
     'L1_ffn_v2': (1.0, 0.6),
     'L1_ffn_bo': (0.0, 0.567)}
    factors = {'L0_mix_Wq': 8.0,
     'L0_mix_Wk': 8.0,
     'L0_mix_Wv': 2.95,
     'L0_mix_Wo': 2.744,
     'L0_ffn_gate_w': 4.44,
     'L0_ffn_W1': 6.345,
     'L0_ffn_W2': 5.957,
     'L1_gnn_weight': 3.048}
    for name, (base, spread) in spreads.items():
        noise = np.random.default_rng([zlib.crc32(name.encode()), seed]).standard_normal(out[name].shape)
        drawn = base * np.exp(spread * noise) if base else spread * noise
        out[name] = jnp.asarray(drawn.astype(out[name].dtype))
    for name, factor in factors.items():
        out[name] = (out[name] * factor).astype(out[name].dtype)
    return out
```

```python
from contextlib import ExitStack, contextmanager

import concourse.bass as bass
from concourse import mybir

F32 = mybir.dt.float32
R32 = mybir.dt.float32r
I32 = mybir.dt.int32
ALU = mybir.AluOpType
ACT = mybir.ActivationFunctionType
AX = mybir.AxisListType

P = 128
D = 256
H = D // P
N = 3125
TP = 125
NT = N // TP
GT = 5
NG = NT // GT
TS = TP + 1
E = 50000
CH = 128
NCH = 400
RW = 100
RR = NCH // RW
CG = 10
NCG = NCH // CG
GC = CG // 2
PR = CG // 2
NPR = NCH // 2
W = 48
WS = 128
NW = 25
NP = NW * WS
MH = 4
MF = 64
TW = 2 * MF + 2 * MH
EPS = 1e-5


class Tally:

    def __init__(self, sem):
        self.sem, self.base, self.n = sem, 0, 0

    def __call__(self, instruction, by=1):
        instruction.then_inc(self.sem, by)
        self.n += by
        return instruction

    @property
    def value(self):
        return self.base + self.n

    def link(self, engine, instruction):
        self(instruction)
        engine.wait_ge(self.sem, self.value)

    def join(self, engine):
        engine.wait_ge(self.sem, self.value)


@contextmanager
def loop(engine, count, *tallies):
    start = [(t.base, t.n) for t, _ in tallies]
    with engine.Fori(0, count) as i:
        for (t, per), (b, n) in zip(tallies, start):
            t.base, t.n = i * per + (b + n), 0
        yield i
        for t, per in tallies:
            assert t.n == per, (t.n, per)
    for (t, per), (b, n) in zip(tallies, start):
        t.base, t.n = b, n + count * per


NL = 4
AH = 8
AD = D // AH
FF = 4 * D
FT = FF // P
NE = 8
MT = 4
SUB = ((0, 3), (3, 2))
A_SCALE = float(AD) ** -0.25

QW = D + 2 * (P + 2)
UC = 2
UB = 5
NU = NCH // UC
SU = NU // (2 * NG)
SB = SU // UB

T_MIX, T_LAYER = NT, 3 * NT
T_MOE = T_MIX + NL * T_LAYER
T_L1 = T_MOE + NT
T_FFN1 = T_L1 + NT
F_LAYER = 2 * FT * NG
F_MOE = NL * F_LAYER
F_RET = F_MOE + NE * NG * 2 * MT
F_FFN1 = F_RET + NG * 2 * 4
Q_MIX, Q_LAYER = NG, 2 * NG
Y_MIX, Y_LAYER = NT, 5 * NT + 2 * NG
Y_MOE = Y_MIX + NL * Y_LAYER
Y_BIAS = Y_MOE + NT
Y_EXP = Y_BIAS + NT
Q_MOE = Q_MIX + NL * Q_LAYER
Q_ROWS = Q_MOE + NG
Q_L1 = Q_ROWS + NG
Q_FFN1 = Q_L1 + NG
Y_L1 = Y_EXP + NE * NT
Y_RET = Y_L1 + 2 * NT
Y_AGG = Y_RET + NT
Y_GATE1 = Y_AGG + NT
Y_BIAS1 = Y_GATE1 + NT
Y_EXP1 = Y_BIAS1 + NT


def gps_kernel(nc, a, out):
    with ExitStack() as ctx:
        build(nc, ctx, a, out)


def build(nc, ctx, a, out):
    def sem(name):
        return ctx.enter_context(nc.semaphore(name))

    def sb(name, shape, dt=F32, scope=ctx):
        return scope.enter_context(nc.sbuf_tensor(name, shape, dt))

    def dram(name, shape, dt=F32):
        return nc.dram_tensor(name, shape, dt).ap()

    table0 = dram("table0", (N, TW))
    table1 = dram("table1", (N, D))
    spill = dram("spill", (NCG, P, CG * MF))

    ident = sb("ident", [P, P])
    blocks = sb("blocks", [P, P])
    ones = sb("ones", [P, P])
    iota_i = sb("iota_i", [P, WS], I32)
    iota = sb("iota", [P, WS])
    z = sb("z", [TP, NT, D])
    srcT = sb("srcT", [P, NCH + 2 * CG], I32)
    relT = sb("relT", [P, NCH + UC])
    restT = sb("restT", [P, NCH])
    base_i = sb("base_i", [1, NPR], I32)
    rest_i = sb("rest_i", [1, 1], I32)
    dinv = sb("dinv", [TP, NT])
    st6 = sb("st6", [TP, GT, 6])
    mv = sb("mv", [TP, GT, 2])
    ve = sb("ve", [TP, GT])
    sd = sb("sd", [TP, GT])
    rstd = sb("rstd", [TP, GT])
    hn = sb("hn", [TP, GT, D])
    hT = [sb(f"hT{k}", [P, H, GT, TS], R32) for k in range(2)]
    gf = sb("gf", [P, 2, 3 * TS])
    act_ = [sb(f"act{k}", [P, 4, 3 * TS], R32) for k in range(2)]

    pa = ctx.enter_context(nc.psum_tensor("pa", [P, 3, 512], F32))
    pb = ctx.enter_context(nc.psum_tensor("pb", [P, 2, 512], F32))
    pt = ctx.enter_context(nc.psum_tensor("pt", [P, 2, 512], F32))
    pg = ctx.enter_context(nc.psum_tensor("pg", [P, 1, 512], F32))

    sg = ExitStack()
    dirT = sb("dirT", [P, 2, NCH], F32, sg)
    score = sb("score", [P, NCH, MH], F32, sg)
    gat = sb("gat", [P, 2, GC, TW], F32, sg)
    m1 = sb("m1", [P, GC, MF], F32, sg)
    m2 = sb("m2", [P, 2, GC, MF], F32, sg)
    sc1 = sb("sc1", [P, 2, GC, MH], F32, sg)
    idx = sb("idx", [P, 2, GC], I32, sg)
    hmax = sb("hmax", [P, MH], F32, sg)
    hm4 = sb("hm4", [MH, 1], F32, sg)
    hd4 = sb("hd4", [MH, MH], F32, sg)
    hmb = sb("hmb", [P, MH], F32, sg)
    s1 = ExitStack()
    x0 = sb("x0", [TP, NT, D], F32, s1)
    src_r = sb("src_r", [RW, RR, CH], I32, s1)
    dst_r = sb("dst_r", [RW, RR, CH], I32, s1)
    attr_r = sb("attr_r", [RW, RR, CH, 2], F32, s1)
    srcf = sb("srcf", [RW, RR, CH], F32, s1)
    dstf = sb("dstf", [RW, RR, CH], F32, s1)
    relf = sb("relf", [RW, RR, CH], F32, s1)
    restf = sb("restf", [RW, RR, CH], F32, s1)
    tmpf = sb("tmpf", [RW, RR, CH], F32, s1)
    basef = sb("basef", [RW, RR // 2], F32, s1)
    rowmax = sb("rowmax", [RW, 1], F32, s1)
    restm = sb("restm", [1, 1], F32, s1)
    wfr = sb("wfr", [MF, 2, D], F32, s1)
    att = sb("att", [MH, MF], F32, s1)
    attT = sb("attT", [MF, MH], F32, s1)
    wcf = sb("wcf", [P, H, TW], F32, s1)
    wcat = [sb(f"wcat{k}", [P, H, TW], R32, s1) for k in range(2)]
    trow = sb("trow", [TP, GT, TW], F32, s1)
    s1.close()
    s3 = ExitStack()
    xin = sb("xin", [TP, NT, D], F32, s3)
    ex = sb("ex", [P, NCH, MH + 1], F32, s3)
    msg = sb("msg", [P, 2, CG, MF], F32, s3)
    wm = sb("wm", [P, 2, CG, MH, MF], F32, s3)
    ex_s = sb("ex_s", [P, 2, CG, MH + 1], F32, s3)
    oh = sb("oh", [P, 2, CG, W], F32, s3)
    ohs = sb("ohs", [P, WS], F32, s3)
    iow = sb("iow", [P, WS], F32, s3)
    acc = sb("acc", [P, 3, NP], F32, s3)
    gout = sb("gout", [TP, D], F32, s3)
    den = sb("den", [TP, 2, MH + 1], F32, s3)
    s3.close()

    s5 = ExitStack()
    qv = sb("qv", [TP, NT, QW], F32, s5)
    s5k = ExitStack()
    kk = sb("kk", [TP, NT, D], F32, s5k)
    s5k.close()
    w2 = [sb(f"w2{k}", [P, FT, D], R32, s5) for k in range(2)]
    over = sb("over", [P, NT * D - 2 * FT * D], F32, s5)
    raw = sb("raw", [P, 2, 4 * D], F32, s5)
    s5w = ExitStack()
    wqkv = [sb(f"wqkv{k}", [P, H, 3 * D], R32, s5w) for k in range(2)]
    s5w.close()
    ks = sb("ks", [TP, 2, D], F32, s5)
    cs = sb("cs", [P, H, P + 2], F32, s5)
    cmT = sb("cmT", [P, H, P], F32, s5)
    mo = [sb(f"mo{k}", [P, H, D], R32, s5) for k in range(2)]
    over2 = sb("over2", [P, 4 * D - 16], F32, s5)
    w1 = [sb(f"w1{k}", [P, H, FF], R32, s5) for k in range(2)]
    wo = sb("wo", [P, H, D], F32, s5)
    lng = sb("lng", [P, 2, H], F32, s5)
    lnb = sb("lnb", [P, 2, H], F32, s5)
    b1c = sb("b1c", [P, FT], F32, s5)
    b1s = sb("b1s", [P, FT], F32, s5)
    bob = sb("bob", [TP, 2, D], F32, s5)
    cm = sb("cm", [P, H, P], F32, s5)
    s5b = ExitStack()
    bqkv = sb("bqkv", [TP, 3 * D], F32, s5b)
    s5b.close()
    kmax = sb("kmax", [TP, D], F32, s5)
    kmaxT = sb("kmaxT", [P, H], F32, s5)
    kmax_end = sb("kmax_end", [TP, 2 * D], F32, s5)
    cr = sb("cr", [P, H], F32, s5)
    qm = sb("qm", [TP, GT, AH], F32, s5)
    qr = sb("qr", [TP, GT, AH], F32, s5)
    s5.close()
    sg.close()

    s6 = ExitStack()
    xT = [sb(f"xT{k}", [P, NG, H, GT * TS], R32, s6) for k in range(2)]
    lg = sb("lg", [TP, NT, NE], F32, s6)
    lgm = sb("lgm", [TP, NT], F32, s6)
    lgb = sb("lgb", [TP, NE], F32, s6)
    gwf = sb("gwf", [P, H, NE], F32, s6)
    gw = [sb(f"gw{k}", [P, H, NE], R32, s6) for k in range(2)]
    cwg = sb("cwg", [TP, 2, GT], F32, s6)
    cws = sb("cws", [TP, GT, NE], F32, s6)
    be_ = sb("be_", [NE, D], F32, s6)
    s6a = ExitStack()
    tri = sb("tri", [TP, NE, NE], F32, s6a)
    cmp = sb("cmp", [TP, 2, NT, NE, NE], F32, s6a)
    rank = sb("rank", [TP, NT, NE], F32, s6a)
    eraw = sb("eraw", [P, 2, 2, 4 * D], F32, s6a)
    ew = [sb(f"ew{k}", [P, 2, 2, 4 * D], R32, s6a) for k in range(2)]
    eb1 = sb("eb1", [P, 2, MT], F32, s6a)
    s6a.close()
    s78 = ExitStack()
    aw = sb("aw", [P, H, D], F32, s78)
    awo = [sb(f"awo{k}", [P, H, D], R32, s78) for k in range(2)]
    bsum = sb("bsum", [TP, 3, D], F32, s78)
    acc1 = sb("acc1", [P, H, NP], F32, s78)
    x_rows = sb("x_rows", [P, UB, UC, D], F32, s78)
    idx1 = sb("idx1", [P, 2, UB, UC], I32, s78)
    oh1 = sb("oh1", [P, UB, UC, W], F32, s78)
    s7 = ExitStack()
    qw = sb("qw", [P, H, 3 * D], F32, s7)
    s7k = ExitStack()
    kvw = [sb(f"kvw{k}", [P, H, 2, D], R32, s7k) for k in range(2)]
    s7k.close()
    rw = [sb(f"rw{k}", [P, H, D], R32, s7) for k in range(2)]
    qT = sb("qT", [P, H, D], F32, s7)
    rw_end = sb("rw_end", [P, H * D], F32, s7)
    bkv = sb("bkv", [TP, 3 * D], F32, s7)
    bq = sb("bq", [P, H], F32, s7)
    lnkv = sb("lnkv", [TP, 2, 2, AD], F32, s7)
    kv = sb("kv", [TP, GT, 2, D], F32, s7)
    kvm = sb("kvm", [TP, GT, 2 * AH], F32, s7)
    s7k = ExitStack()
    kvq = sb("kvq", [TP, GT, 2, D], F32, s7k)
    s7k.close()
    s7k = ExitStack()
    awr = sb("awr", [P, H, D], F32, s7k)
    s7k.close()
    mw = [sb(f"mw{k}", [P, 2 * H, D], R32, s7) for k in range(2)]
    mw_end = sb("mw_end", [P, GT * 2 * D - 4 * H * D], F32, s7)
    kva = sb("kva", [P, H, P], F32, s7)
    rwf = sb("rwf", [P, H, D], F32, s7)
    rb = sb("rb", [P, H], F32, s7)
    mraw = sb("mraw", [P, 2 * H, D], F32, s7)
    mb1 = sb("mb1", [P, H], F32, s7)
    s7.close()
    s8 = ExitStack()
    g1 = sb("g1", [TP, NT, D], F32, s8)
    ss = sb("ss", [TP, NT], F32, s8)
    ohs1 = sb("ohs1", [P, WS], F32, s8)
    iow1 = sb("iow1", [P, WS], F32, s8)
    s8.close()
    s78.close()
    s9 = ExitStack()
    act9 = [sb(f"act9{k}", [P, 6, 3 * TS], R32, s9) for k in range(2)]
    fraw = sb("fraw", [P, 2, 3 * H, D], F32, s9)
    fw = [sb(f"fw{k}", [P, 2, 3 * H, D], R32, s9) for k in range(2)]
    bnp = sb("bnp", [P, 2, 5, NE * H], F32, s9)
    bns = sb("bns", [P, NE, 4, H], F32, s9)
    bne = sb("bne", [P, 2, 4, H], F32, s9)
    s9.close()
    s6.close()

    wbank = [pa[:, 0], pa[:, 1], pa[:, 2], pb[:, 0], pb[:, 1]]

    unit_banks = [[pa[:, i] for i in range(3)], [pt[:, i] for i in range(2)]]
    UNIT_FREE = (1, 0)
    kv_banks = [pg[:, 0], pb[:, 1]]
    ret_banks = [pg[:, 0], pt[:, 0]]

    s = {}
    for n in ("stage x_ld edge_ld w_ld const pool_w act_w dve_w dve_go act_go pe_go "
              "mvr sdr hn_ready t_ps t_hi t_lo y_ps y_used row_st "
              "idx_ready settle_DVE settle_PE settle_Pool settle_SP settle_Activation gat0 gat1 msg_ready msg_st0 msg_st1 "
              "msg_ld0 msg_ld1 msg_used wm_ready win_ps win_used "
              "g_ps g_used out_st "
              "up_ps gf_done f_hi f_lo act_used raw_ld0 raw_ld1 raw_used par_ld par_used act5 pe5 dve5 ks_ready ks_used q_ready q_exp "
              "xin_ld xT_ready p6_ld lg_go ex_go cw_go e_ld0 e_ld1 e_split e_ready "
              "t1_st rows_ready p7_ld kv_go sq_go kv_ready pe7 dve7 g7 "
              "ra_ld ra_in ra_used ra_oh ra_mm ra_w rb_ld rb_in rb_used rb_oh rb_mm rb_w rb_sum "
              "cwt cwg_in ix1 rw0 rw1 rw2 rw3 rw4 rw_used o1_ready "
              "p9_ld f_ld0 f_ld1 f_split bn_go act9").split():
        s[n] = sem(n)

    block = ctx.enter_context(nc.Block())
    xg = a["x"].rearrange("(g t p) d -> g p t d", g=NG, p=TP)
    og = out.rearrange("(g t p) d -> g p t d", g=NG, p=TP)

    def stage_end(eng, n):
        eng.drain().then_inc(s["stage"], 1)
        eng.wait_ge(s["stage"], 5 * n)

    def settle(eng):
        eng.sem_inc(s["settle_" + eng.engine.name], 1)

    def slot_free(t, j):
        return t + (2, 0, 1, 1, 1)[j]

    def hi_lo_products(ps, lhs, rhs, first=True, last=True):
        for n, (l, r) in enumerate(((0, 0), (0, 1), (1, 0))):
            mm = nc.tensor.matmul(ps, lhs(l), rhs(r), start=first and n == 0, stop=last and n == 2)
        return mm

    def rest_flag(eng):
        return eng.value_load(rest_i[0:1, 0:1], min_val=0, max_val=1)

    @block.sync
    def _(sp):
        for g in range(NG):
            sp.dma_start(x0[:, g * GT:(g + 1) * GT, :], xg[g]).then_inc(s["x_ld"], 16)
        sp.dma_start(wfr[:, 0, :], a["L0_gnn_W_forward"]).then_inc(s["w_ld"], 16)
        sp.dma_start(wfr[:, 1, :], a["L0_gnn_W_reverse"]).then_inc(s["w_ld"], 16)
        sp.dma_start(att[:, :], a["L0_gnn_attn_forward"][0]).then_inc(s["w_ld"], 16)
        row = RR * CH
        full = E // row
        part = E - full * row
        for to, flat, k in ((src_r[:, :, :].rearrange("p r e -> p (r e)"), a["src"], 1),
                            (attr_r[:, :, :, :].rearrange("p r e c -> p (r e c)"),
                             a["edge_attr_2"].rearrange("e c -> (e c)"), 2)):
            sp.dma_start(to[0:full, :], flat[0:full * row * k].rearrange("(p e) -> p e", p=full)).then_inc(s["edge_ld"], 16)
            sp.dma_start(to[full:full + 1, 0:part * k], flat[full * row * k:E * k].rearrange("(p e) -> p e", p=1)).then_inc(s["edge_ld"], 16)
            sp.dma_start(to[full:full + 1, part * k:row * k], flat[0:(row - part) * k].rearrange("(p e) -> p e", p=1)).then_inc(s["edge_ld"], 16)
            sp.dma_start(to[full + 1:RW, :], flat[0:(RW - full - 1) * row * k].rearrange("(p e) -> p e", e=row * k)).then_inc(s["edge_ld"], 16)
        sp.wait_ge(s["const"], 1)
        to = dst_r[:, :, :].rearrange("p r e -> p (r e)")
        sp.dma_start(to[0:full, :], a["dst"][0:full * row].rearrange("(p e) -> p e", p=full)).then_inc(s["edge_ld"], 16)
        sp.dma_start(to[full:full + 1, 0:part], a["dst"][full * row:E].rearrange("(p e) -> p e", p=1)).then_inc(s["edge_ld"], 16)
        t0 = table0.rearrange("(g t p) c -> g p t c", g=NG, p=TP)
        with sp.Fori(0, NG) as g:
            sp.wait_ge(s["y_used"], g * GT + GT + 3)
            sp.dma_start(t0[bass.ds(g, 1)].rearrange("o p t c -> p (o t) c"), trow[:, :, :]).then_inc(s["row_st"], 16)
        sp.wait_ge(s["row_st"], 16 * NG + 16)
        stage_end(sp, 1)
        def store_messages(first):
            with sp.Fori(0, NG) as i:
                for b in range(2):
                    sp.wait_ge(s["msg_ready"], (first + i) * 2 + (b + 2))
                    sp.dma_start(spill[bass.ds(first + i, 1)].rearrange("o p c -> p (o c)")[:, b * GC * MF:(b + 1) * GC * MF],
                                 m2[:, b].rearrange("p c f -> p (c f)")).then_inc(s[f"msg_st{b}"], 16)

        with sp.Fori(0, NL) as l:
            def of(name):
                return a["L0_mix_" + name][bass.ds(l, 1)]
            sp.wait_ge(s["par_used"], l + 1)
            for n, name in enumerate(("ln1", "ln2")):
                sp.dma_start(lng[:, n, :], of(name + "_g").rearrange("o (h p) -> p (o h)", p=P),
                             allow_slow_non_contiguous=True).then_inc(s["par_ld"], 16)
                sp.dma_start(lnb[:, n, :], of(name + "_b").rearrange("o (h p) -> p (o h)", p=P),
                             allow_slow_non_contiguous=True).then_inc(s["par_ld"], 16)
            sp.dma_start(b1c[:, :], of("b1").rearrange("o (h p) -> p (o h)", p=P),
                             allow_slow_non_contiguous=True).then_inc(s["par_ld"], 16)
            for n, name in enumerate(("bo", "b2")):
                sp.dma_start(bob[:, n, :], of(name).to_broadcast([TP, D])).then_inc(s["par_ld"], 16)
            sp.dma_start(wo[:, :, :], of("Wo").rearrange("o (h p) n -> p (o h) n", p=P)).then_inc(s["par_ld"], 16)
            for pair in range(3):
                if pair == 2:
                    store_messages(l * (2 * NG))
                for h in range(2):
                    sp.wait_ge(s["raw_used"], l * 3 + pair + 1)
                    sem_ = s[f"raw_ld{h}"]
                    if pair == 0:
                        for k, name in enumerate(("Wq", "Wk", "Wv")):
                            sp.dma_start(raw[:, h, k * D:(k + 1) * D],
                                         of(name)[:, h * P:(h + 1) * P, :].rearrange("o p n -> p (o n)")).then_inc(sem_, 16)
                    elif pair == 1:
                        sp.dma_start(raw[:, h, :], of("W1")[:, h * P:(h + 1) * P, :].rearrange("o p n -> p (o n)")).then_inc(sem_, 16)
                    else:
                        sp.dma_start(raw[:, h, :].rearrange("p (c n) -> p c n", n=D),
                                     of("W2")[:, h * 4 * P:(h + 1) * 4 * P, :].rearrange("o (c p) n -> p (o c) n", p=P)).then_inc(sem_, 16)
            store_messages(l * (2 * NG) + NG)
        for b in range(2):
            sp.wait_ge(s[f"msg_st{b}"], 16 * (NCG + 1))
        stage_end(sp, 2)
        sp.dma_start(xin[:, :, :], a["x"].rearrange("(t p) d -> p t d", p=TP)).then_inc(s["xin_ld"], 16)
        stage_end(sp, 3)
        with sp.Fori(0, NCG // 2) as i:
            for b in range(2):
                sp.wait_ge(s["msg_used"], i * 2 + b + 1)
                sp.dma_start(msg[:, b].rearrange("p c f -> p (c f)"),
                             spill[bass.ds(i * 2 + b, 1)].rearrange("o p c -> p (o c)")).then_inc(s[f"msg_ld{b}"], 16)
        with sp.If(rest_flag(sp) == 1):
            sp.wait_ge(s["msg_used"], NCG + 2)
            with sp.Fori(0, NCG) as n:
                sp.wait_ge(s["ra_used"], n + 1)
                sp.dma_start(msg[:, 0].rearrange("p c f -> p (c f)"),
                             spill[bass.ds(n, 1)].rearrange("o p c -> p (o c)")).then_inc(s["ra_ld"], 16)
        stage_end(sp, 4)
        stage_end(sp, 5)
        sp.dma_start(gwf[:, :, :], a["L0_ffn_gate_w"].rearrange("(h p) e -> p h e", p=P)).then_inc(s["p6_ld"], 16)
        sp.dma_start(lgb[:, :], a["L0_ffn_gate_b"].rearrange("(o e) -> o e", o=1).to_broadcast([TP, NE])).then_inc(s["p6_ld"], 16)
        sp.dma_start(be_[:, :], a["L0_ffn_b2"]).then_inc(s["p6_ld"], 16)
        with sp.Fori(0, NE // 2) as ep:
            for b in range(2):
                e = ep * 2 + b
                sp.wait_ge(s["e_split"], e + 1)
                sp.wait_ge(s["gf_done"], F_MOE + 2 - NG * 2 * MT + e * (NG * 2 * MT))
                sp.dma_start(eraw[:, b, 0, :].rearrange("p (h n) -> p h n", h=H),
                             a["L0_ffn_W1"][bass.ds(e, 1)].rearrange("o (h p) n -> p (o h) n", p=P)).then_inc(s[f"e_ld{b}"], 16)
                sp.dma_start(eraw[:, b, 1, :].rearrange("p (c n) -> p c n", n=D),
                             a["L0_ffn_W2"][bass.ds(e, 1)].rearrange("o (c p) n -> p (o c) n", p=P)).then_inc(s[f"e_ld{b}"], 16)
                sp.dma_start(eb1[:, b, :], a["L0_ffn_b1"][bass.ds(e, 1)].rearrange("o (c p) -> p (o c)", p=P),
                             allow_slow_non_contiguous=True).then_inc(s[f"e_ld{b}"], 16)
        stage_end(sp, 6)
        t1 = table1.rearrange("(g t p) c -> g p t c", g=NG, p=TP)
        with sp.Fori(0, NG) as g:
            sp.wait_ge(s["rows_ready"], g + 1)
            sp.dma_start(t1[bass.ds(g, 1)].rearrange("o p t c -> p (o t) c"), kv[:, :, 0, :]).then_inc(s["t1_st"], 16)
        def p7(out_, in_, slow=False):
            sp.dma_start(out_, in_, allow_slow_non_contiguous=slow).then_inc(s["p7_ld"], 16)
        p7(qw[:, :, :], a["L1_mix_w_qkv"].rearrange("(h p) n -> p h n", p=P))
        p7(bkv[:, :], a["L1_mix_b_qkv"].rearrange("(o n) -> o n", o=1).to_broadcast([TP, 3 * D]))
        for h in range(AH):
            p7(bq[h % 4 * AD:h % 4 * AD + AD, h // 4:h // 4 + 1],
               a["L1_mix_b_qkv"][h * 3 * AD:h * 3 * AD + AD].rearrange("(p o) -> p o", o=1), True)
        for n, name in enumerate("kv"):
            p7(lnkv[:, n, 0, :], a[f"L1_mix_{name}ln_g"].rearrange("(o n) -> o n", o=1).to_broadcast([TP, AD]))
            p7(lnkv[:, n, 1, :], a[f"L1_mix_{name}ln_b"].rearrange("(o n) -> o n", o=1).to_broadcast([TP, AD]))
        p7(awr[:, :, :], a["L1_gnn_weight"][0:D].rearrange("(h p) n -> p h n", p=P))
        p7(aw[:, :, :], a["L1_gnn_weight"][D:2 * D].rearrange("(h p) n -> p h n", p=P))
        p7(mraw[:, 0:H, :], a["L1_mix_w1"].rearrange("(h p) n -> p h n", p=P))
        p7(mraw[:, H:2 * H, :], a["L1_mix_w2"].rearrange("(h p) n -> p h n", p=P))
        p7(mb1[:, :], a["L1_mix_b1"].rearrange("(h p) -> p h", p=P), True)
        p7(bsum[:, 0, :], a["L1_mix_b2"].rearrange("(o n) -> o n", o=1).to_broadcast([TP, D]))
        p7(bsum[:, 1, :], a["L1_gnn_bias"].rearrange("(o n) -> o n", o=1).to_broadcast([TP, D]))
        stage_end(sp, 7)
        stage_end(sp, 8)
        def p9(out_, in_, slow=False):
            sp.dma_start(out_, in_, allow_slow_non_contiguous=slow).then_inc(s["p9_ld"], 16)
        p9(gwf[:, :, :], a["L1_ffn_Wr"].rearrange("(h p) e -> p h e", p=P))
        p9(lgb[:, :], a["L1_ffn_br"].rearrange("(o e) -> o e", o=1).to_broadcast([TP, NE]))
        p9(be_[:, :], a["L1_ffn_bo"])
        for n in range(2):
            for k, name in enumerate(("g", "be", "m", "v", "b")):
                p9(bnp[:, n, k, :], a[f"L1_ffn_{name}{n + 1}"].rearrange("e (h p) -> p (e h)", p=P), True)
        with sp.Fori(0, NE // 2) as ep:
            for b in range(2):
                e = ep * 2 + b
                sp.wait_ge(s["f_split"], e + 1)
                for k, name in enumerate(("W1", "W2", "Wo")):
                    sp.dma_start(fraw[:, b, k * H:(k + 1) * H, :],
                                 a["L1_ffn_" + name][bass.ds(e, 1)].rearrange("o (h p) n -> p (o h) n", p=P)).then_inc(s[f"f_ld{b}"], 16)
        for g in range(NG):
            sp.wait_ge(s["y_used"], Y_EXP1 + NE * NT - NT + (g + 1) * GT + 3)
            sp.dma_start(og[g], z[:, g * GT:(g + 1) * GT, :]).then_inc(s["out_st"], 16)
        sp.wait_ge(s["out_st"], 16 * NG)
        stage_end(sp, 9)

    @block.gpsimd
    def _(pool):
        me = Tally(s["pool_w"])
        me(nc.gpsimd.memset(ident[:, :], 0.0))
        me(nc.gpsimd.memset(blocks[:, :], 1.0))
        nc.gpsimd.memset(dst_r[:, :, :], -1).then_inc(s["const"], 1)
        me(nc.gpsimd.memset(ones[:, :], 1.0))
        me(nc.gpsimd.iota(iota_i[:, :], pattern=[[1, WS]], base=0, channel_multiplier=0))
        me.join(pool)
        me(nc.gpsimd.affine_select(out=ident[:, :], in_=ident[:, :], compare_op=ALU.not_equal, fill=1.0,
                                   base=0, pattern=[[-1, P]], channel_multiplier=1))
        bl = blocks[:, :].rearrange("p (b e) -> p b e", e=32)
        me(nc.gpsimd.affine_select(out=bl, in_=bl, compare_op=ALU.is_ge, fill=0.0,
                                   base=0, pattern=[[-32, 4], [0, 32]], channel_multiplier=1))
        me.join(pool)
        me(nc.gpsimd.affine_select(out=bl, in_=bl, compare_op=ALU.is_ge, fill=0.0,
                                   base=31, pattern=[[32, 4], [0, 32]], channel_multiplier=-1))
        for k in range(2):
            me(nc.gpsimd.memset(hT[k][:, :, :, :].bitcast(F32), 0.0))
        me.join(pool)
        pool.nop().then_inc(s["const"], 1)
        stage_end(pool, 1)
        nc.gpsimd.memset(qv[:, :, D:QW], 1.0).then_inc(s["const"], 1)
        def fetch(slot, b):
            pool.wait_ge(s["idx_ready"], slot * 2 + (b + 1))
            settle(pool)
            for c in range(GC):
                pool.indirect_dma_start(out=gat[:, b, c, :], out_offset=None, in_=table0,
                                        in_offset=bass.IndirectOffsetOnAxis(ap=idx[:, b, c:c + 1], axis=0)
                                        ).then_inc(s[f"gat{b}"], 16)

        for b in range(2):
            fetch(0, b)
        with pool.Fori(1, NCG) as slot:
            for b in range(2):
                fetch(slot, b)
        stage_end(pool, 2)
        nc.gpsimd.memset(acc[:, :, :], 0.0).then_inc(s["const"], 1)
        stage_end(pool, 3)
        stage_end(pool, 4)
        stage_end(pool, 5)

        def keep_tiles(t0, g):
            pool.wait_ge(s["t_lo"], t0 + (GT + 2))
            for k in range(2):
                nc.gpsimd.tensor_copy(xT[k][:, bass.ds(g, 1)].rearrange("p o h c -> p (o h) c"),
                                      hT[k][:, :, :, :].rearrange("p h t c -> p h (t c)")).then_inc(s["xT_ready"], 1)

        def split_expert(raw_, halves, loaded, value, used, used_value, raw_used, ready):
            pool.wait_ge(loaded, value)
            pool.wait_ge(used, used_value)
            settle(pool)
            me(nc.gpsimd.tensor_copy(halves[0], raw_))
            me.join(pool)
            me(nc.gpsimd.tensor_tensor(halves[1], raw_, halves[0], ALU.subtract))
            me.join(pool)
            pool.nop().then_inc(raw_used, 1)
            pool.nop().then_inc(ready, 1)

        me(nc.gpsimd.memset(tri[:, :, :], 1.0))
        me.join(pool)
        me(nc.gpsimd.affine_select(out=tri[:, :, :], in_=tri[:, :, :], compare_op=ALU.is_ge, fill=0.0,
                                   base=-1, pattern=[[1, NE], [-1, NE]], channel_multiplier=0))
        me.join(pool)
        pool.nop().then_inc(s["const"], 1)
        pool.nop().then_inc(s["e_split"], 2)
        with pool.Fori(0, NG) as g:
            keep_tiles(g * GT + T_MOE, g)
        with loop(pool, NE // 2, (me, 4)) as ep:
            for b in range(2):
                e = ep * 2 + b
                split_expert(eraw[:, b], [w[:, b] for w in ew], s[f"e_ld{b}"], ep * 48 + 48,
                             s["act_used"], F_MOE + 4 - NG * 2 * MT + e * (NG * 2 * MT), s["e_split"], s["e_ready"])
        stage_end(pool, 6)
        me(nc.gpsimd.memset(acc1[:, :, :], 0.0))
        me.join(pool)
        pool.nop().then_inc(s["const"], 1)
        pool.wait_ge(s["t1_st"], 16 * NG + 16)

        def fetch_rows(first, k):
            for b in range(UB):
                if b == 0:
                    pool.wait_ge(s["ix1"], first + k + 1)
                pool.wait_ge(s["rw_used"], first * UB + (k * UB + b + 1))
                settle(pool)
                for c in range(UC):
                    pool.indirect_dma_start(out=x_rows[:, b, c, :], out_offset=None, in_=table1,
                                            in_offset=bass.IndirectOffsetOnAxis(ap=idx1[:, k % 2, b, c:c + 1], axis=0)
                                            ).then_inc(s[f"rw{b}"], 16)

        with pool.Fori(0, NG) as g:
            fetch_rows(g * SB, 0)
            fetch_rows(g * SB, 1)
            keep_tiles(g * GT + T_L1, g)
            fetch_rows(g * SB, 2)
            fetch_rows(g * SB, 3)
        with pool.Fori(NG, 2 * NG) as g:
            for k in range(SB):
                fetch_rows(g * SB, k)
        stage_end(pool, 7)
        with pool.If(rest_flag(pool) == 1):
            with pool.Fori(0, NU) as n:
                pool.wait_ge(s["rb_in"], n + 1)
                settle(pool)
                for c in range(UC):
                    pool.indirect_dma_start(out=x_rows[:, 0, c, :], out_offset=None, in_=table1,
                                            in_offset=bass.IndirectOffsetOnAxis(ap=idx1[:, 0, 0, c:c + 1], axis=0)
                                            ).then_inc(s["rb_ld"], 16)
        stage_end(pool, 8)
        pool.nop().then_inc(s["f_split"], 2)
        with pool.Fori(0, NG) as g:
            keep_tiles(g * GT + T_FFN1, g)
        with loop(pool, NE // 2, (me, 4)) as ep:
            for b in range(2):
                e = ep * 2 + b
                split_expert(fraw[:, b], [w[:, b] for w in fw], s[f"f_ld{b}"], ep * 48 + 48,
                             s["y_used"], Y_EXP1 + 3 - NT + e * NT, s["f_split"], s["e_ready"])
        stage_end(pool, 9)

    @block.tensor
    def _(pe):
        def transposes(t, j, src):
            pe.wait_ge(s["hn_ready"], t + 2)
            pe.wait_ge(s["t_hi"], slot_free(t, j))
            pe.wait_ge(s["t_lo"], slot_free(t, j))
            for h in range(H):
                last = nc.tensor.transpose(pt[:, j % 2, h * P:h * P + TP], src[:, h * P:(h + 1) * P],
                                           ident[0:TP, 0:TP])
            last.then_inc(s["t_ps"], 1)

        def wait_tile(t):
            pe.wait_ge(s["t_lo"], t + 3)

        def y_product(y, k, j, rhs, cols=D, free=1):
            pe.wait_ge(s["y_used"], y + free)
            for h in range(H):
                last = hi_lo_products(pa[0:TP, k, 0:cols], lambda l: hT[l][:, h, j, 0:TP],
                                      lambda r: rhs(r, h), h == 0, h == H - 1)
            last.then_inc(s["y_ps"], 1)
            return last

        pe.nop().then_inc(s["act_used"], 4)
        pe.nop().then_inc(s["t_ps"], GT)
        pe.wait_ge(s["const"], 2)
        pe.wait_ge(s["w_ld"], 48)
        for w in range(2):
            for h in range(H):
                nc.tensor.transpose(pb[:, 0, (w * H + h) * MF:(w * H + h + 1) * MF],
                                    wfr[:, w, h * P:(h + 1) * P], ident[0:MF, 0:MF])
        nc.tensor.transpose(pb[0:MF, 1, 0:MH], att[:, :], ident[0:MH, 0:MH]).then_inc(s["pe_go"], 1)
        pe.wait_ge(s["dve_go"], 1)
        for w in range(2):
            for h in range(H):
                last = nc.tensor.matmul(pb[:, 1, 8 + (w * H + h) * MH:8 + (w * H + h + 1) * MH],
                                        wfr[:, w, h * P:(h + 1) * P], attT[:, :], start=True, stop=True)
        last.then_inc(s["pe_go"], 1)
        pe.wait_ge(s["dve_go"], 3)
        for r in range(RR):
            pe.wait_ge(s["dve_go"], 3 + r)
            for k, rows in enumerate((srcf[:, r], relf[:, r], restf[:, r], attr_r[:, r, :, 0])):
                nc.tensor.transpose(pb[:, 0, k * RW:(k + 1) * RW], rows, ident[0:RW, 0:RW])
            nc.tensor.transpose(pb[:, 1, 0:RW], attr_r[:, r, :, 1], ident[0:RW, 0:RW])
            nc.tensor.transpose(pb[0:1, 1, P:P + RW], basef[:, r // 2:r // 2 + 1], ident[0:RW, 0:RW]).then_inc(s["pe_go"], 1)
        pe.wait_ge(s["dve_go"], 3 + RR)
        nc.tensor.transpose(pb[0:1, 1, 256:256 + RW], rowmax[:, :], ident[0:RW, 0:RW]).then_inc(s["pe_go"], 1)
        with pe.Fori(0, NG) as g:
            for j in range(GT):
                transposes(g * GT + j, j, hn[:, j])
            for j in range(GT):
                wait_tile(g * GT + j)
                y_product(g * GT + j, j % 3, j, lambda r, h: wcat[r][:, h, :], TW, (2, 2, 1, 1, 1)[j])
        stage_end(pe, 1)

        def up(F, f, n, lhs, rhs, parts=H):
            pe.wait_ge(s["gf_done"], F + 1)
            for k in range(parts):
                last = hi_lo_products(pb[:, f % 2, 0:n], lambda l: lhs(l, k), lambda r: rhs(r, k), k == 0, k == parts - 1)
            return last.then_inc(s["up_ps"], 1)

        def down(F, f, tiles, rhs, first, last, banks=unit_banks[0]):
            pe.wait_ge(s["f_lo"], F + 3)
            for i in range(tiles):
                mm = hi_lo_products(banks[i][0:TP, 0:D], lambda l: act_[l][:, f % 4, i * TS:i * TS + TP], rhs, first, last)
                if last and i < tiles - 1:
                    mm.then_inc(s["y_ps"], 1)
            mm.then_inc(s["act_used"], 1)

        def tiles_of(u, k, r):
            first, n = SUB[u]
            return hT[r][:, k, first:first + n, :].rearrange("p t c -> p (t c)")

        pe.nop().then_inc(s["raw_used"], 1)
        with pe.Fori(0, NL) as l:
            T, Y, F = l * T_LAYER + T_MIX, l * Y_LAYER + Y_MIX, l * F_LAYER
            pe.wait_ge(s["dve5"], l * 9 + 1)
            for h in range(2):
                pe.wait_ge(s[f"raw_ld{h}"], l * 80 + 48)
            for k in range(3):
                for h in range(H):
                    last = nc.tensor.matmul(pa[0:TP, k, 0:D], cm[:, h, 0:TP], raw[:, h, k * D:(k + 1) * D],
                                            start=h == 0, stop=h == H - 1)
            last.then_inc(s["pe5"], 1)
            pe.wait_ge(s["dve5"], l * 9 + 2)
            settle(pe)
            with pe.Fori(0, NG) as g:
                for j in range(GT):
                    transposes(T + g * GT + j, j, hn[:, j])
                for j in range(GT):
                    wait_tile(T + g * GT + j)
                    for k in range(3):
                        y_product(Y + (g * GT + j) * 3 + k, k, j, lambda r, h: wqkv[r][:, h, k * D:(k + 1) * D])
            for h in range(2):
                pe.wait_ge(s[f"raw_ld{h}"], l * 80 + 64)
            pe.wait_ge(s["gf_done"], F + 2)
            for f in range(FT):
                for h in range(H):
                    last = nc.tensor.matmul(pb[:, 0, f:f + 1], raw[:, h, f * P:(f + 1) * P], lnb[:, 1, h:h + 1],
                                            start=h == 0, stop=h == H - 1)
            last.then_inc(s["pe5"], 1)
            pe.wait_ge(s["dve5"], l * 9 + 4)
            for h in range(H):
                last = nc.tensor.transpose(pb[:, 1, h * P:h * P + TP], kmax[:, h * P:(h + 1) * P], ident[0:TP, 0:TP])
            last.then_inc(s["pe5"], 1)
            pe.wait_ge(s["dve5"], l * 9 + 5)
            for h in range(H):
                last = nc.tensor.matmul(pb[0:TP, 1, h * P:(h + 1) * P], ones[:, 0:TP], cm[:, h, :], start=True, stop=True)
            last.then_inc(s["pe5"], 1)
            with pe.Fori(0, NG) as g:
                pe.wait_ge(s["y_used"], Y + g * 2 + (3 * NT + 3))
                for j in range(GT):
                    pe.wait_ge(s["act5"], l * NT + g * GT + j + 1)
                    for h in range(H):
                        last = nc.tensor.matmul(pa[:, h, 0:P + 1], ks[:, j % 2, h * P:(h + 1) * P],
                                                qv[:, bass.ds(g * GT + j, 1), D + h * (P + 2):D + h * (P + 2) + P + 1].rearrange("p o c -> p (o c)"),
                                                start=j == 0, stop=j == GT - 1)
                    last.then_inc(s["ks_used"], 1)
                pe.wait_ge(s["ks_used"], l * NT + g * GT + GT + 2)
                pe.nop().then_inc(s["y_ps"], 2)
            pe.wait_ge(s["dve5"], l * 9 + 6)
            for h in range(H):
                last = nc.tensor.transpose(pb[:, 0, h * P:(h + 1) * P], cm[:, h, :], ident[:, :])
            last.then_inc(s["pe5"], 1)
            pe.wait_ge(s["dve5"], l * 9 + 7)
            for h in range(H):
                last = nc.tensor.matmul(pb[:, 1, h * D:(h + 1) * D], cmT[:, h, :], wo[:, h, :], start=True, stop=True)
            last.then_inc(s["pe5"], 1)
            pe.wait_ge(s["dve5"], l * 9 + 8)
            settle(pe)
            with pe.Fori(0, NG) as g:
                Tq, Yq, Fg = T + NT + g * (2 * GT), Y + (3 * NT + 2 * NG) + g * (2 * GT), F + g * (2 * FT)
                for j in range(GT):
                    transposes(Tq + j, j, hn[:, j])
                for j in range(GT):
                    wait_tile(Tq + j)
                    y_product(Yq + j, j % 3, j, lambda r, h: mo[r][:, h, :], free=(2, 2, 1, 1, 1)[j])
                for j in range(GT):
                    transposes(Tq + GT + j, j, hn[:, j])
                wait_tile(Tq + 2 * GT - 1)
                units = [(u, f) for u in range(2) for f in range(FT)]
                for n, (u, f) in enumerate(units):
                    if n == 0:
                        up(Fg, 0, SUB[0][1] * TS, lambda l_, k: w1[l_][:, k, 0:P], lambda r, k: tiles_of(0, k, r))
                    if n + 1 < len(units):
                        u1, f1 = units[n + 1]
                        up(Fg + n + 1, n + 1, SUB[u1][1] * TS, lambda l_, k: w1[l_][:, k, f1 * P:(f1 + 1) * P],
                                lambda r, k: tiles_of(u1, k, r))
                    if f == 0:
                        pe.wait_ge(s["y_used"], Yq + GT + SUB[u][0] + 3)
                    down(Fg + n, n, SUB[u][1], lambda r: w2[r][:, f, :], f == 0, f == FT - 1)
        stage_end(pe, 2)
        pe.wait_ge(s["dve_go"], 5 + RR)
        nc.tensor.transpose(pb[0:MH, 0, 0:P], hmax[:, :], ident[:, :]).then_inc(s["pe_go"], 1)
        pe.wait_ge(s["dve_go"], 6 + RR)
        nc.tensor.matmul(pb[:, 1, 0:MH], ones[0:MH, :], hd4[:, :], start=True, stop=True).then_inc(s["pe_go"], 1)
        stage_end(pe, 3)
        with pe.Fori(0, NCG // 2) as i:
            for b in range(2):
                pe.wait_ge(s["wm_ready"], i * 2 + b + 1)
                for q in range(PR):
                    pe.wait_ge(s["win_used"], (i * 2 + b) * PR + (q + 1))
                    o = wbank[q][:, 0:3 * W].rearrange("p (k n) -> p k n", k=3)
                    for k in range(3):
                        for c in (2 * q, 2 * q + 1):
                            rows, part = (P, wm[:, b, c, 2 * k:2 * k + 2].rearrange("p k f -> p (k f)")) if k < 2 else (MH + 1, ex_s[:, b, c, :])
                            last = nc.tensor.matmul(o[0:rows, k], part, oh[:, b, c, :], start=c == 2 * q, stop=c == 2 * q + 1)
                    last.then_inc(s["win_ps"], 1)
        with pe.If(rest_flag(pe) == 1):
            pe.wait_ge(s["win_used"], NPR + PR)
            with pe.Fori(0, NCG * NW) as w:
                for c in range(CG):
                    pe.wait_ge(s["ra_oh"], w * CG + (c + 1))
                    for k in range(2):
                        nc.tensor.matmul(pb[:, k, 0:WS], wm[:, 0, c, 2 * k:2 * k + 2].rearrange("p k f -> p (k f)"),
                                         ohs[:, :], start=c == 0, stop=c == CG - 1)
                    nc.tensor.matmul(pg[0:MH + 1, 0, 0:WS], ex_s[:, 0, c, :], ohs[:, :],
                                     start=c == 0, stop=c == CG - 1).then_inc(s["ra_mm"], 1)
        stage_end(pe, 4)
        for t in range(NT):
            if t >= 2:
                pe.wait_ge(s["g_used"], t - 1)
            for k in range(2):
                nc.tensor.transpose(pa[0:TP, t % 2, k * P:(k + 1) * P], acc[:, k, t * TP:(t + 1) * TP], ident[:, :])
            nc.tensor.transpose(pa[0:TP, t % 2, 2 * P:2 * P + MH + 1], acc[0:MH + 1, 2, t * TP:(t + 1) * TP],
                                ident[0:MH + 1, 0:MH + 1]).then_inc(s["g_ps"], 1)
        stage_end(pe, 5)

        def gates(t0, y0):
            with pe.Fori(0, NG) as g:
                for j in range(GT):
                    transposes(g * GT + (t0 + j), j, hn[:, j])
                for j in range(GT):
                    wait_tile(g * GT + (t0 + j))
                    y_product(g * GT + (y0 + j), j % 3, j, lambda r, h: gw[r][:, h, :], NE, (2, 2, 1, 1, 1)[j])

        def bias_terms(y0, n0):
            with pe.Fori(0, NG) as g:
                pe.wait_ge(s["cw_go"], g * 2 + (n0 + 1))
                for j in range(GT):
                    last = nc.tensor.transpose(pb[0:NE, j // 4, j % 4 * P:j % 4 * P + TP], cws[:, j, :], ident[0:TP, 0:TP])
                last.then_inc(s["lg_go"], 1)
                pe.wait_ge(s["cw_go"], g * 2 + (n0 + 2))
                for j in range(GT):
                    pe.wait_ge(s["y_used"], g * GT + (y0 + j) + (2, 2, 1, 1, 1)[j])
                    nc.tensor.matmul(pa[0:TP, j % 3, 0:D], hn[0:NE, j, 0:TP], be_[:, :], start=True, stop=True).then_inc(s["y_ps"], 1)

        def x_cols(g, u, k, r):
            first, n = SUB[u]
            return xT[r][:, bass.ds(g, 1) if not isinstance(g, int) else slice(g, g + 1), k,
                         first * TS:(first + n) * TS].rearrange("p o c -> p (o c)")

        pe.wait_ge(s["const"], 5)
        pe.wait_ge(s["dve5"], 9 * NL + 1)
        gates(T_MOE, Y_MOE)
        bias_terms(Y_BIAS, 0)
        pe.wait_ge(s["xT_ready"], 2 * NG + 1)
        pe.wait_ge(s["y_used"], Y_EXP + 3)

        def expert_up(e, b, g, u, f):
            if f == 0 and u == 0:
                pe.wait_ge(s["e_ready"], e + 1)
            up(((e * NG + g) * 2 + u) * MT + (F_MOE + f), f, SUB[u][1] * TS,
               lambda l, k: ew[l][:, b, 0, (k * MT + f) * P:(k * MT + f + 1) * P], lambda r, k: x_cols(g, u, k, r))

        def expert_group(e, b, g, nxt):
            units = [(u, f) for u in range(2) for f in range(MT)]
            for n, (u, f) in enumerate(units):
                if n + 1 < len(units):
                    expert_up(e, b, g, *units[n + 1])
                elif nxt:
                    expert_up(*nxt, 0, 0)
                if f == 0:
                    pe.wait_ge(s["y_used"], (e * NG + g) * GT + (Y_EXP + SUB[u][0] + UNIT_FREE[u]))
                down((e * NG + g) * (2 * MT) + (F_MOE + n), f, SUB[u][1],
                     lambda r: ew[r][:, b, 1, f * D:(f + 1) * D], f == 0, f == MT - 1, unit_banks[u])

        def expert_pair(ep, last):
            for b in range(2):
                e = ep * 2 + b
                with pe.Fori(0, NG - 1) as g:
                    expert_group(e, b, g, (e, b, g + 1))
                expert_group(e, b, NG - 1, None if last and b else (e + 1, 1 - b, 0))

        expert_up(0, 0, 0, 0, 0)
        with pe.Fori(0, NE // 2 - 1) as ep:
            expert_pair(ep, False)
        expert_pair(NE // 2 - 1, True)
        stage_end(pe, 6)
        def unit_windows(slot, units, banks):
            for k in units:
                b = k % UB
                pe.wait_ge(s[f"rw{b}"], slot * (SB * 16 * UC) + (k // UB + 1) * (16 * UC))
                pe.wait_ge(s["o1_ready"], slot * SU + (k + 1))
                pe.wait_ge(s["win_used"], slot * SU + (NPR + PR - 1 + k))
                for h in range(H):
                    for c in range(UC):
                        last = nc.tensor.matmul(banks[k % 2][:, h * W:(h + 1) * W], x_rows[:, b, c, h * P:(h + 1) * P],
                                                oh1[:, b, c, :], start=c == 0, stop=c == UC - 1)
                last.then_inc(s["win_ps"], 1)

        pe.wait_ge(s["dve7"], 1)
        with pe.Fori(0, NG) as g:
            unit_windows(g, range(0, 4), kv_banks)
            for j in range(GT):
                transposes(g * GT + (T_L1 + j), j, hn[:, j])
            unit_windows(g, range(4, 6), kv_banks)
            for j in range(GT):
                wait_tile(g * GT + (T_L1 + j))
                for k in range(2):
                    n = 2 * j + k
                    y_product(g * (2 * GT) + (Y_L1 + n), n % 3, j, lambda r, h: kvw[r][:, h, k, :], free=3 if n == 0 else 1)
                if j % 2:
                    unit_windows(g, (6 + j // 2,), kv_banks)
            unit_windows(g, range(8, SU), kv_banks)
            pe.wait_ge(s["kv_ready"], g + 1)
            for h in range(H):
                for j in range(GT):
                    last = nc.tensor.matmul(pb[:, 0, h * P:(h + 1) * P], kv[:, j, 0, h * P:(h + 1) * P], kv[:, j, 1, h * P:(h + 1) * P],
                                            start=j == 0, stop=j == GT - 1)
            last.then_inc(s["g7"], 1)
        for h in range(H):
            for k in range(H):
                last = nc.tensor.transpose(pt[:, h, k * P:(k + 1) * P], rwf[:, k, h * P:(h + 1) * P], ident[:, :])
        last.then_inc(s["pe7"], 1)
        pe.wait_ge(s["dve7"], 3)
        for h in range(H):
            for k in range(H):
                nc.tensor.matmul(pa[:, k, h * P:(h + 1) * P], qT[:, h, k * P:(k + 1) * P], kva[:, h, :], start=True, stop=True)
        for h in range(H):
            last = nc.tensor.matmul(pa[:, 2, h:h + 1], kva[:, h, :], bq[:, h:h + 1], start=True, stop=True)
        last.then_inc(s["pe7"], 1)
        pe.wait_ge(s["dve7"], 4)
        pe.wait_ge(s["xT_ready"], 4 * NG + 1)
        with pe.Fori(0, NG) as g:
            for u in range(2):
                F = (g * 2 + u) * 4 + F_RET
                n = SUB[u][1] * TS
                for f in range(2):
                    up(F + f, f, n, lambda l, k: rw[l][:, k, f * P:(f + 1) * P], lambda r, k: x_cols(g, u, k, r))
                unit_windows(g + NG, range(u * 10, u * 10 + 4), ret_banks)
                pe.wait_ge(s["f_lo"], F + 4)
                for f in range(2):
                    up(F + 2 + f, f, n, lambda l, k: mw[l][:, k, f * P:(f + 1) * P], lambda r, k: act_[r][:, k, 0:n])
                pe.wait_ge(s["up_ps"], F + 4)
                pe.nop().then_inc(s["act_used"], 2)
                pe.wait_ge(s["y_used"], g * GT + (Y_RET + SUB[u][0] + 3))
                unit_windows(g + NG, range(u * 10 + 4, u * 10 + 8), ret_banks)
                for f in range(2):
                    down(F + 2 + f, 2 + f, SUB[u][1], lambda r: mw[r][:, H + f, :], f == 0, f == 1)
                unit_windows(g + NG, range(u * 10 + 8, u * 10 + 10), ret_banks)
        stage_end(pe, 7)
        with pe.If(rest_flag(pe) == 1):
            with pe.Fori(0, NU * NW) as w:
                for c in range(UC):
                    pe.wait_ge(s["rb_oh"], w * UC + (c + 1))
                    for h in range(H):
                        last = nc.tensor.matmul(pb[:, h, 0:WS], x_rows[:, 0, c, h * P:(h + 1) * P], ohs1[:, :],
                                                start=c == 0, stop=c == UC - 1)
                    last.then_inc(s["rb_mm"], 1)
            pe.wait_ge(s["rb_sum"], 1)
        for t in range(NT):
            pe.wait_ge(s["y_used"], Y_AGG + t + 2)
            for h in range(H):
                hi_lo_products(pb[0:TP, t % 2, 0:D], lambda l: xT[l][:, t // GT, h, t % GT * TS:t % GT * TS + TP],
                               lambda r: awo[r][:, h, :], h == 0, h == H - 1)
            for h in range(H):
                last = nc.tensor.matmul(pa[0:TP, t % 3, 0:D], acc1[:, h, t * TP:(t + 1) * TP], aw[:, h, :],
                                        start=h == 0, stop=h == H - 1)
            last.then_inc(s["y_ps"], 1)
        stage_end(pe, 8)
        pe.wait_ge(s["dve7"], 5)
        gates(T_FFN1, Y_GATE1)
        bias_terms(Y_BIAS1, 2 * NG)
        pe.wait_ge(s["xT_ready"], 6 * NG + 1)
        pe.wait_ge(s["y_used"], Y_EXP1 + 3)

        def unit_a(e, b, g, u, F):
            if u == 0:
                pe.wait_ge(s["e_ready"], e + (NE + 1))
            for f in range(2):
                up(F + f, f, SUB[u][1] * TS, lambda l, k: fw[l][:, b, k, f * P:(f + 1) * P], lambda r, k: x_cols(g, u, k, r))

        def unit_b(b, u, F, Fa):
            pe.wait_ge(s["f_lo"], Fa + 4)
            n = SUB[u][1] * TS
            for f in range(2):
                up(F + f, f, n, lambda l, k: fw[l][:, b, H + k, f * P:(f + 1) * P], lambda r, k: act9[r][:, 2 * u + k, 0:n])
            pe.wait_ge(s["up_ps"], F + 2)
            pe.nop().then_inc(s["act_used"], 2)

        def unit_d(b, u, Fb, y):
            pe.wait_ge(s["f_lo"], Fb + 4)
            pe.wait_ge(s["y_used"], y + UNIT_FREE[u])
            tiles = SUB[u][1]
            for i in range(tiles):
                for k in range(H):
                    mm = hi_lo_products(unit_banks[u][i][0:TP, 0:D], lambda l: act9[l][:, 4 + k, i * TS:i * TS + TP],
                                        lambda r: fw[r][:, b, 2 * H + k, :], k == 0, k == H - 1)
                if i < tiles - 1:
                    mm.then_inc(s["y_ps"], 1)
            mm.then_inc(s["act_used"], 2)

        def step(e, b, g, u, nxt, prev, n):
            if nxt:
                unit_a(*nxt, n * 4 + (F_FFN1 + 2))
            if prev:
                unit_d(*prev)
            unit_b(b, u, n * 4 + (F_FFN1 + (4 if nxt else 2)), n * 4 + (F_FFN1 - 2) if not (isinstance(n, int) and n == 0) else F_FFN1)

        def ffn_expert(e, b, first, last):
            def two(g, head, tail):
                n = (e * NG + g) * 2
                y = (e * NG + g) * GT + Y_EXP1
                pb_ = (1 - b) if head else b
                step(e, b, g, 0, (e, b, g, 1), None if head and first else (pb_, 1, n * 4 + F_FFN1, y - SUB[1][1]), n)
                step(e, b, g, 1, (None if last else (e + 1, 1 - b, 0, 0)) if tail else (e, b, g + 1, 0),
                     (b, 0, n * 4 + (F_FFN1 + 4), y), n + 1)
            two(0, True, False)
            with pe.Fori(1, NG - 1) as g:
                two(g, False, False)
            two(NG - 1, False, True)

        unit_a(0, 0, 0, 0, F_FFN1)
        ffn_expert(0, 0, True, False)
        with pe.Fori(0, NE // 2 - 1) as ep:
            ffn_expert(ep * 2 + 1, 1, False, False)
            ffn_expert(ep * 2 + 2, 0, False, False)
        ffn_expert(NE - 1, 1, False, True)
        n = NE * NG * 2
        unit_d(1, 1, n * 4 + (F_FFN1 - 2), Y_EXP1 + NE * NT - SUB[1][1])
        stage_end(pe, 9)

    @block.scalar
    def _(act):
        def root(q):
            act.wait_ge(s["mvr"], q + 1)
            nc.scalar.activation(sd[:, :], ve[:, :], ACT.Sqrt).then_inc(s["sdr"], 1)

        def upper(t, j, y, F=None, kept=None):
            act.wait_ge(s["t_ps"], t + 1 + GT)
            if y is not None:
                act.wait_ge(s["y_ps"], y)
            if F is not None:
                act.wait_ge(s["gf_done"], F + 2)
            if kept is not None:
                act.wait_ge(s["xT_ready"], kept + 1)
            nc.scalar.activation(hT[0][:, :, j, 0:TP],
                                 pt[:, j % 2, 0:H * P].rearrange("p (h c) -> p h c", h=H)[:, :, 0:TP],
                                 ACT.Copy).then_inc(s["t_hi"], 1)

        act.nop().then_inc(s["t_hi"], 2)
        act.nop().then_inc(s["gf_done"], 2)
        act.nop().then_inc(s["f_hi"], 2)
        with act.Fori(0, NG) as g:
            root(g)
            for j in range(GT):
                act.wait_ge(s["y_used"], g * GT + 3)
                upper(g * GT + j, j, None)
        stage_end(act, 1)

        def hidden(F, f, n, func, bias, scale=1.0):
            act.wait_ge(s["up_ps"], F + 1)
            act.wait_ge(s["f_lo"], F + 1)
            act.wait_ge(s["f_hi"], F + 1)
            nc.scalar.activation(gf[:, f % 2, 0:n], pb[:, f % 2, 0:n], func, bias=bias, scale=scale).then_inc(s["gf_done"], 1)
            act.wait_ge(s["gf_done"], F + 3)
            act.wait_ge(s["act_used"], F + 1)
            nc.scalar.activation(act_[0][:, f % 4, 0:n], gf[:, f % 2, 0:n], ACT.Copy).then_inc(s["f_hi"], 1)

        with act.Fori(0, NL) as l:
            T, Y, F, Q = l * T_LAYER + T_MIX, l * Y_LAYER + Y_MIX, l * F_LAYER, l * Q_LAYER + Q_MIX
            root(Q)
            with act.Fori(0, NG - 1) as g:
                for j in range(GT):
                    upper(T + g * GT + j, j, Y + g * (3 * GT), F)
                root(Q + (g + 1))
            for j in range(GT):
                upper(T + ((NG - 1) * GT + j), j, Y + (NG - 1) * (3 * GT), F)
            with act.Fori(0, NG) as g:
                for j in range(GT):
                    act.wait_ge(s["ks_ready"], l * NT + g * GT + j + 1)
                    nc.scalar.activation(ks[:, j % 2, :], ks[:, j % 2, :], ACT.Exp, scale=A_SCALE).then_inc(s["act5"], 1)
            def q_exp(g):
                act.wait_ge(s["q_ready"], l * NG + g + 1)
                nc.scalar.activation(hn[:, :, :], hn[:, :, :], ACT.Exp, scale=A_SCALE).then_inc(s["q_exp"], 1)

            def ffn_group(g, ahead):
                Tq, Fg = T + NT + g * (2 * GT), F + g * (2 * FT)
                for j in range(GT):
                    upper(Tq + j, j, Y + (3 * NT + 2 * NG), Fg)
                root(Q + NG + g)
                for j in range(GT):
                    upper(Tq + GT + j, j, Y + (3 * NT + 2 * NG) + g * (2 * GT) + (j + 1))
                for u in range(2):
                    for f in range(FT):
                        hidden(Fg + u * FT + f, f, SUB[u][1] * TS, ACT.Gelu, b1s[:, f:f + 1])
                        if u == 0 and f == GT and ahead:
                            q_exp(g + 1)

            q_exp(0)
            with act.Fori(0, NG - 1) as g:
                ffn_group(g, True)
            ffn_group(NG - 1, False)
        stage_end(act, 2)
        act.wait_ge(s["dve_go"], 7 + RR)
        nc.scalar.activation(ex[:, :, 0:MH], score[:, :, :], ACT.Exp).then_inc(s["act_go"], 1)
        stage_end(act, 3)
        stage_end(act, 4)
        stage_end(act, 5)

        def norm_group(q0, t0, y0, kept, per=1):
            with act.Fori(0, NG) as g:
                root(g + q0)
                for j in range(GT):
                    upper(g * GT + (t0 + j), j, g * (per * GT) + y0, None, g * 2 + kept)

        norm_group(Q_MOE, T_MOE, Y_MOE, 0)
        act.wait_ge(s["ex_go"], 1)
        nc.scalar.activation(lg[:, :, :], lg[:, :, :], ACT.Exp).then_inc(s["ex_go"], 1)
        with act.Fori(0, NE // 2) as ep:
            for b in range(2):
                e = ep * 2 + b
                act.wait_ge(s[f"e_ld{b}"], ep * 48 + 48)
                settle(act)
                with act.Fori(0, NG) as g:
                    for u in range(2):
                        for f in range(MT):
                            hidden(((e * NG + g) * 2 + u) * MT + (F_MOE + f), f, SUB[u][1] * TS, ACT.Gelu, eb1[:, b, f:f + 1])
        stage_end(act, 6)
        with act.Fori(0, NG) as g:
            root(g + Q_ROWS)
        with act.Fori(0, NG) as g:
            root(g + Q_L1)
            for j in range(GT):
                upper(g * GT + (T_L1 + j), j, g * (2 * GT) + Y_L1, None, g * 2 + 2 * NG)
            act.wait_ge(s["kv_go"], g * 2 + 1)
            nc.scalar.activation(kvq[:, :, :, :], kv[:, :, :, :], ACT.Square).then_inc(s["sq_go"], 1)
            act.wait_ge(s["kv_go"], g * 2 + 2)
            nc.scalar.activation(kvm[:, :, :], kvm[:, :, :], ACT.Sqrt).then_inc(s["sq_go"], 1)
        with act.Fori(0, NG) as g:
            for u in range(2):
                F = (g * 2 + u) * 4 + F_RET
                for f in range(2):
                    hidden(F + f, f, SUB[u][1] * TS, ACT.Identity, rb[:, f:f + 1])
                for f in range(2):
                    hidden(F + 2 + f, 2 + f, SUB[u][1] * TS, ACT.Gelu, mb1[:, f:f + 1])
        stage_end(act, 7)
        for t in range(NT):
            act.wait_ge(s["y_used"], Y_AGG + t + 4)
            if t:
                act.wait_ge(s["act9"], t)
            nc.scalar.activation(hn[:, 0, :], g1[:, t, :], ACT.Square, accum_out=ss[:, t:t + 1]).then_inc(s["act9"], 1)
        act.wait_ge(s["act9"], NT)
        nc.scalar.activation(ss[:, :], ss[:, :], ACT.Sqrt).then_inc(s["act9"], 1)
        stage_end(act, 8)
        act.wait_ge(s["bn_go"], 1)
        nc.scalar.activation(bnp[:, :, 3, :], bnp[:, :, 3, :], ACT.Sqrt).then_inc(s["bn_go"], 1)
        norm_group(Q_FFN1, T_FFN1, Y_GATE1, 4 * NG)
        act.wait_ge(s["ex_go"], 3)
        nc.scalar.activation(lg[:, :, :], lg[:, :, :], ACT.Exp).then_inc(s["ex_go"], 1)
        act.wait_ge(s["bn_go"], 3)

        def hidden9(F, f, slot, n, bias, scale, free):
            act.wait_ge(s["up_ps"], F + 1)
            act.wait_ge(s["f_lo"], F + 1)
            act.wait_ge(s["f_hi"], F + 1)
            nc.scalar.activation(gf[:, f % 2, 0:n], pb[:, f % 2, 0:n], ACT.Relu, bias=bias, scale=scale).then_inc(s["gf_done"], 1)
            act.wait_ge(s["gf_done"], F + 3)
            act.wait_ge(s["act_used"], free)
            nc.scalar.activation(act9[0][:, slot, 0:n], gf[:, f % 2, 0:n], ACT.Copy).then_inc(s["f_hi"], 1)

        def load_norms(e, b):
            act.wait_ge(s["gf_done"], e * (NG * 8) + (F_FFN1 + 2 - NG * 8 + 2))
            nc.scalar.activation(bne[:, b, :, :].rearrange("p k h -> p (k h)"),
                                 bns[:, bass.ds(e, 1) if not isinstance(e, int) else slice(e, e + 1), :, :].rearrange("p o k h -> p (o k h)"),
                                 ACT.Copy).then_inc(s["act9"], 1)
            act.wait_ge(s["act9"], e + (NT + 2))

        def act_a(b, u, F, n):
            for f in range(2):
                hidden9(F + f, f, 2 * u + f, SUB[u][1] * TS, bne[:, b, 1, f:f + 1], bne[:, b, 0, f:f + 1],
                        n * 4 + (F_FFN1 + 4 - 6))

        def act_b(b, u, n, end=False):
            for f in range(2):
                hidden9(n * 4 + (F_FFN1 + (2 if end else 4) + f), f, 4 + f, SUB[u][1] * TS, bne[:, b, 3, f:f + 1], bne[:, b, 2, f:f + 1],
                        n * 4 + (F_FFN1 + 4))

        def act_expert(e, b, last):
            def two(g, tail):
                n = (e * NG + g) * 2
                act_a(b, 1, n * 4 + (F_FFN1 + 2), n + 1)
                act_b(b, 0, n)
                if not tail:
                    act_a(b, 0, n * 4 + (F_FFN1 + 6), n + 2)
                elif not last:
                    load_norms(e + 1, 1 - b)
                    act_a(1 - b, 0, n * 4 + (F_FFN1 + 6), n + 2)
                act_b(b, 1, n + 1, tail and last)
            with act.Fori(0, NG - 1) as g:
                two(g, False)
            two(NG - 1, True)

        load_norms(0, 0)
        act_a(0, 0, F_FFN1, 0)
        act_expert(0, 0, False)
        with act.Fori(0, NE // 2 - 1) as ep:
            act_expert(ep * 2 + 1, 1, False)
            act_expert(ep * 2 + 2, 0, False)
        act_expert(NE - 1, 1, True)
        stage_end(act, 9)

    @block.vector
    def _(dve):
        me = Tally(s["dve_w"])

        def norm_stats(t0, src):
            dve.wait_ge(s["hn_ready"], t0 + 1)
            settle(dve)
            for j in range(GT):
                me(nc.vector.bn_stats(st6[:, j, :], src(j)))
            me.join(dve)
            settle(dve)
            for j in range(GT):
                me(nc.vector.bn_aggr(mv[:, j, :], st6[:, j, :]))
            me.join(dve)
            nc.vector.tensor_scalar(ve[:, :], mv[:, :, 1], EPS, None, ALU.add).then_inc(s["mvr"], 1)

        def norm_apply(q, t0, src):
            dve.wait_ge(s["sdr"], q + 1)
            me.link(dve, nc.vector.reciprocal(rstd[:, :], sd[:, :]))
            for j in range(GT):
                dve.wait_ge(s["t_ps"], t0 + j + 1)
                nc.vector.tensor_scalar(hn[:, j, :], src(j), mv[:, j, 0:1], rstd[:, j:j + 1],
                                        ALU.subtract, ALU.mult).then_inc(s["hn_ready"], 1)

        def norm(q, t0, src):
            norm_stats(t0, src)
            norm_apply(q, t0, src)

        def lower(t, j):
            dve.wait_ge(s["t_hi"], t + 3)
            nc.vector.tensor_tensor(hT[1][:, :, j, 0:TP],
                                    pt[:, j % 2, 0:H * P].rearrange("p (h c) -> p h c", h=H)[:, :, 0:TP],
                                    hT[0][:, :, j, 0:TP], ALU.subtract).then_inc(s["t_lo"], 1)

        dve.nop().then_inc(s["hn_ready"], 1)
        for n in ("row_st", "t1_st"):
            dve.nop().then_inc(s[n], 16)
        for n in ("msg_ready", "xT_ready", "g7"):
            dve.nop().then_inc(s[n], 1)
        dve.nop().then_inc(s["t_lo"], 2)
        dve.nop().then_inc(s["f_lo"], 2)
        dve.nop().then_inc(s["y_used"], 3)
        dve.wait_ge(s["pe_go"], 1)
        nc.vector.tensor_copy(attT[:, :], pb[0:MF, 1, 0:MH]).then_inc(s["dve_go"], 1)
        for w in range(2):
            for h in range(H):
                me(nc.vector.tensor_copy(wcf[:, h, w * MF:(w + 1) * MF], pb[:, 0, (w * H + h) * MF:(w * H + h + 1) * MF]))
        dve.wait_ge(s["pe_go"], 2)
        for w in range(2):
            for h in range(H):
                me(nc.vector.tensor_copy(wcf[:, h, 2 * MF + w * MH:2 * MF + (w + 1) * MH],
                                         pb[:, 1, 8 + (w * H + h) * MH:8 + (w * H + h + 1) * MH]))
        me.join(dve)
        me.link(dve, nc.vector.tensor_copy(wcat[0][:, :, :], wcf[:, :, :]))
        nc.vector.tensor_tensor(wcat[1][:, :, :], wcf[:, :, :], wcat[0][:, :, :], ALU.subtract).then_inc(s["dve_go"], 1)
        dve.wait_ge(s["edge_ld"], 16 * 10)
        dve.wait_ge(s["const"], 2)
        me(nc.vector.tensor_copy(iota[:, :], iota_i[:, :]))
        me(nc.vector.tensor_copy(srcf[:, :, :], src_r[:, :, :]))
        me.link(dve, nc.vector.tensor_copy(dstf[:, :, :], dst_r[:, :, :]))
        me.link(dve, nc.vector.tensor_scalar(basef[:, :], dstf[:, 0:RR:2, 0], 0.0, float(N - 1), ALU.max, ALU.min))
        me.link(dve, nc.vector.tensor_tensor(relf[:, :, :].rearrange("p (a b) e -> p a (b e)", b=2),
                                             dstf[:, :, :].rearrange("p (a b) e -> p a (b e)", b=2),
                                             basef[:, :].unsqueeze(2).to_broadcast([RW, RR // 2, 2 * CH]), ALU.subtract))
        me(nc.vector.tensor_scalar(restf[:, :, :], relf[:, :, :], 0.0, None, ALU.is_lt))
        me(nc.vector.tensor_scalar(tmpf[:, :, :], relf[:, :, :], float(W), None, ALU.is_ge))
        me.join(dve)
        me.link(dve, nc.vector.tensor_tensor(restf[:, :, :], restf[:, :, :], tmpf[:, :, :], ALU.add))
        me.link(dve, nc.vector.scalar_tensor_tensor(restf[:, :, :].rearrange("p r e -> p (r e)"),
                                                    dstf[:, :, :].rearrange("p r e -> p (r e)"), 1.0,
                                                    restf[:, :, :].rearrange("p r e -> p (r e)"), ALU.add, ALU.mult))
        me.link(dve, nc.vector.tensor_scalar(restf[:, :, :], restf[:, :, :], -1.0, None, ALU.add))
        me.link(dve, nc.vector.tensor_scalar(tmpf[:, :, :], restf[:, :, :], float(N) - 0.5, None, ALU.is_lt))
        me.link(dve, nc.vector.tensor_tensor(tmpf[:, :, :], tmpf[:, :, :], restf[:, :, :], ALU.mult))
        me(nc.vector.tensor_reduce(rowmax[:, :], tmpf[:, :, :].rearrange("p r e -> p (r e)"), AX.X, ALU.max))
        me.join(dve)
        nc.vector.tensor_scalar(rowmax[:, :], rowmax[:, :], -1.0, 1.0, ALU.max, ALU.add).then_inc(s["dve_go"], 1)
        for r in range(RR):
            dve.wait_ge(s["pe_go"], 3 + r)
            cols = slice(r, NCH, RR)
            me(nc.vector.tensor_copy(srcT[:, cols], pb[:, 0, 0:RW]))
            me(nc.vector.tensor_copy(relT[:, cols], pb[:, 0, RW:2 * RW]))
            me(nc.vector.tensor_copy(restT[:, cols], pb[:, 0, 2 * RW:3 * RW]))
            me(nc.vector.tensor_copy(dirT[:, 0, cols], pb[:, 0, 3 * RW:4 * RW]))
            me(nc.vector.tensor_copy(dirT[:, 1, cols], pb[:, 1, 0:RW]))
            nc.vector.tensor_copy(base_i[:, r // 2:NPR:RR // 2], pb[0:1, 1, P:P + RW]).then_inc(s["dve_go"], 1)
        dve.wait_ge(s["pe_go"], 3 + RR)
        me.link(dve, nc.vector.tensor_reduce(restm[:, :], pb[0:1, 1, 256:256 + RW], AX.X, ALU.max))
        nc.vector.tensor_scalar(rest_i[:, :], restm[:, :], 0.5, None, ALU.is_gt).then_inc(s["dve_go"], 1)
        dve.wait_ge(s["x_ld"], 16 * NG)
        with loop(dve, NG, (me, 3 * GT + 1)) as g:
            norm(g, g * GT, lambda j: x0[:, bass.ds(g * GT + j, 1), :].rearrange("p o d -> p (o d)"))
            dve.wait_ge(s["hn_ready"], g * GT + GT + 1)
            for j in range(GT):
                me(nc.vector.tensor_copy(z[:, bass.ds(g * GT + j, 1), :].rearrange("p o d -> p (o d)"), hn[:, j, :]))
            for j in range(GT):
                lower(g * GT + j, j)
            dve.wait_ge(s["row_st"], g * 16 + 16)
            for j in range(GT):
                dve.wait_ge(s["y_ps"], g * GT + j + 1)
                nc.vector.tensor_copy(trow[:, j, :], pa[0:TP, j % 3, 0:TW]).then_inc(s["y_used"], 1)
        stage_end(dve, 1)

        def zt(t, n=1):
            part = z[:, t:t + n, :] if isinstance(t, int) else z[:, bass.ds(t, n), :]
            return part.rearrange("p o d -> p (o d)") if n == 1 else part

        def tile_of(x, t, lo, hi):
            part = x[:, t:t + 1, lo:hi] if isinstance(t, int) else x[:, bass.ds(t, 1), lo:hi]
            return part.rearrange("p o c -> p (o c)")

        def lower_f(F, f, n):
            dve.wait_ge(s["f_hi"], F + 3)
            nc.vector.tensor_tensor(act_[1][:, f % 4, 0:n], gf[:, f % 2, 0:n], act_[0][:, f % 4, 0:n],
                                    ALU.subtract).then_inc(s["f_lo"], 1)

        def add_y(y, k, out_ap, in_ap, F=None):
            if F is None:
                dve.wait_ge(s["y_ps"], y + 1)
            else:
                dve.wait_ge(s["act_used"], F + 5)
                dve.nop().then_inc(s["y_ps"], 1)
            nc.vector.tensor_tensor(out_ap, pa[0:TP, k, 0:D], in_ap, ALU.add).then_inc(s["y_used"], 1)

        def split(out_, in_, scale=None):
            if scale is None:
                me.link(dve, nc.vector.tensor_copy(out_[0], in_))
                me(nc.vector.tensor_tensor(out_[1], in_, out_[0], ALU.subtract))
            else:
                me.link(dve, nc.vector.tensor_scalar(out_[0], in_, scale, None, ALU.mult))
                me(nc.vector.scalar_tensor_tensor(out_[1], in_, scale, out_[0], ALU.mult, ALU.subtract))

        def messages(slot, parts=(0, 1)):
            for b in parts:
                n = slot * 2 + b
                dve.wait_ge(s[f"gat{b}"], slot * (16 * GC) + 16 * GC)
                dve.wait_ge(s[f"msg_st{b}"], slot * 16 + 16)
                dve.wait_ge(s["msg_ready"], n + 1)
                me.join(dve)
                for k, m in enumerate((m1[:, :, :], m2[:, b])):
                    weight = dirT[:, k, bass.ds(n * GC, GC)].unsqueeze(2)
                    me(nc.vector.tensor_tensor(m, gat[:, b, :, k * MF:(k + 1) * MF], weight.to_broadcast([P, GC, MF]), ALU.mult))
                    me(nc.vector.tensor_tensor(sc1[:, k], gat[:, b, :, 2 * MF + k * MH:2 * MF + (k + 1) * MH],
                                               weight.to_broadcast([P, GC, MH]), ALU.mult))
                me.join(dve)
                nc.vector.tensor_copy(idx[:, b, :], srcT[:, bass.ds((n + 2) * GC, GC)]).then_inc(s["idx_ready"], 1)
                nc.vector.tensor_tensor(m2[:, b], m2[:, b], m1[:, :, :], ALU.add).then_inc(s["msg_ready"], 1)
                me(nc.vector.tensor_tensor(score[:, bass.ds(n * GC, GC), :], sc1[:, 0], sc1[:, 1], ALU.add))

        for b in range(2):
            dve.nop().then_inc(s[f"msg_st{b}"], 16)
        me(nc.vector.memset(srcT[:, NCH:NCH + 2 * CG], 0))
        me(nc.vector.memset(relT[:, NCH:NCH + UC], -1.0))
        for b in range(2):
            nc.vector.tensor_copy(idx[:, b, :], srcT[:, b * GC:(b + 1) * GC]).then_inc(s["idx_ready"], 1)
        me.join(dve)
        dve.wait_ge(s["const"], 3)
        dve.nop().then_inc(s["par_used"], 1)
        dve.nop().then_inc(s["ks_used"], 2)
        PER_G1 = 2 * GT + 1 + 10
        PER_G3 = 2 * GT + 3 + 10 + 4 * GT
        with loop(dve, NL, (me, 33 + NG * (PER_G1 + PER_G3))) as l:
            T, Y, F, Q = l * T_LAYER + T_MIX, l * Y_LAYER + Y_MIX, l * F_LAYER, l * Q_LAYER + Q_MIX
            dve.wait_ge(s["par_ld"], l * 128 + 128)
            for h in range(H):
                me(nc.vector.tensor_scalar(cm[:, h, :], ones[:, :], lnb[:, 0, h:h + 1], None, ALU.mult))
            me.join(dve)
            dve.nop().then_inc(s["dve5"], 1)
            for h in range(H):
                dve.wait_ge(s[f"raw_ld{h}"], l * 80 + 48)
                split([w[:, h, :] for w in wqkv], raw[:, h, 0:3 * D], lng[:, 0, h:h + 1])
            dve.wait_ge(s["pe5"], l * 6 + 1)
            for k in range(3):
                me(nc.vector.tensor_copy(bqkv[:, k * D:(k + 1) * D], pa[0:TP, k, 0:D]))
            me.join(dve)
            dve.nop().then_inc(s["raw_used"], 1)
            dve.nop().then_inc(s["dve5"], 1)
            settle(dve)
            def qkv_group(g, ahead):
                for j in range(GT):
                    lower(T + g * GT + j, j)
                for j in range(GT):
                    for k in range(3):
                        src = pa[0:TP, k, 0:D]
                        bias = bqkv[:, k * D:(k + 1) * D]
                        if k < 2:
                            dst = tile_of(qv if k == 0 else kk, g * GT + j, 0, D)
                        else:
                            dst = tile_of(qv, g * GT + j, D, QW).rearrange("p (h c) -> p h c", h=H)[:, :, 0:P]
                            src = src.rearrange("p (h c) -> p h c", h=H)
                            bias = bias.rearrange("p (h c) -> p h c", h=H)
                        dve.wait_ge(s["y_ps"], Y + (g * GT + j) * 3 + k + 1)
                        nc.vector.tensor_tensor(dst, src, bias, ALU.add).then_inc(s["y_used"], 1)
                    if j == 0 and ahead:
                        norm_stats(T + (g + 1) * GT, lambda i: zt((g + 1) * GT + i))
                    if j == 1:
                        messages(l * (2 * NG) + g, (0,))
                    if j == 2 and ahead:
                        norm_apply(Q + (g + 1), T + (g + 1) * GT, lambda i: zt((g + 1) * GT + i))
                    if j == 3:
                        messages(l * (2 * NG) + g, (1,))

            norm(Q, T, zt)
            with loop(dve, NG - 1, (me, PER_G1)) as g:
                qkv_group(g, True)
            qkv_group(NG - 1, False)
            for h in range(H):
                dve.wait_ge(s[f"raw_ld{h}"], l * 80 + 64)
                split([w[:, h, :] for w in w1], raw[:, h, :], lng[:, 1, h:h + 1])
            dve.wait_ge(s["pe5"], l * 6 + 2)
            me(nc.vector.tensor_tensor(b1s[:, :], pb[:, 0, 0:FT], b1c[:, :], ALU.add))
            me.join(dve)
            dve.nop().then_inc(s["raw_used"], 1)
            dve.nop().then_inc(s["dve5"], 1)
            dve.wait_ge(s["y_used"], Y + 3 * NT + 3)
            nc.vector.tensor_reduce(kmax[:, :], kk[:, :, :].rearrange("p t f -> p f t"), AX.X, ALU.max).then_inc(s["dve5"], 1)
            dve.wait_ge(s["pe5"], l * 6 + 3)
            me.link(dve, nc.vector.tensor_reduce(kmaxT[:, :], pb[:, 1, 0:D].rearrange("p (h c) -> p h c", h=H)[:, :, 0:TP], AX.X, ALU.max))
            for h in range(H):
                me(nc.vector.tensor_scalar(cm[:, h, :], ident[:, :], kmaxT[:, h:h + 1], None, ALU.mult))
            me.join(dve)
            dve.nop().then_inc(s["dve5"], 1)
            dve.wait_ge(s["pe5"], l * 6 + 4)
            me(nc.vector.tensor_copy(kmax[:, :], pb[0:TP, 1, 0:D]))
            me.link(dve, nc.vector.memset(cs[:, :, :], 0.0))
            settle(dve)
            with loop(dve, NG, (me, 1)) as g:
                for j in range(GT):
                    dve.wait_ge(s["ks_used"], slot_free(l * NT + g * GT + j, j))
                    nc.vector.tensor_tensor(ks[:, j % 2, :], kk[:, bass.ds(g * GT + j, 1), :].rearrange("p o d -> p (o d)"),
                                            kmax[:, :], ALU.subtract).then_inc(s["ks_ready"], 1)
                dve.wait_ge(s["y_ps"], Y + 3 * NT + g * 2 + 2)
                me.join(dve)
                me.link(dve, nc.vector.tensor_tensor(cs[:, :, 0:P + 1], cs[:, :, 0:P + 1], pa[:, 0:H, 0:P + 1], ALU.add))
                dve.nop().then_inc(s["y_used"], 2)
            me.link(dve, nc.vector.reciprocal(cr[:, :], cs[:, :, P]))
            for h in range(H):
                me(nc.vector.scalar_tensor_tensor(cm[:, h, :], cs[:, h, 0:P], cr[:, h:h + 1], blocks[:, :], ALU.mult, ALU.mult))
            me.join(dve)
            dve.nop().then_inc(s["dve5"], 1)
            dve.wait_ge(s["pe5"], l * 6 + 5)
            nc.vector.tensor_copy(cmT[:, :, :], pb[:, 0, 0:H * P].rearrange("p (h c) -> p h c", h=H)).then_inc(s["dve5"], 1)
            dve.wait_ge(s["pe5"], l * 6 + 6)
            split([m[:, :, :] for m in mo], pb[:, 1, :].rearrange("p (h c) -> p h c", h=H))
            for h in range(H):
                dve.wait_ge(s[f"raw_ld{h}"], l * 80 + 80)
                split([w[:, 4 * h:4 * h + 4, :] for w in w2], raw[:, h, :].rearrange("p (c n) -> p c n", n=D))
            me.join(dve)
            dve.nop().then_inc(s["raw_used"], 1)
            dve.nop().then_inc(s["dve5"], 1)
            def by_head(x):
                return x.rearrange("p (h c) -> p h c", h=AH)

            def q_shift(g, j):
                q_ = by_head(tile_of(qv, g * GT + j, 0, D))
                me.link(dve, nc.vector.tensor_reduce(qm[:, j, :], q_, AX.X, ALU.max))
                dve.wait_ge(s["t_ps"], T + NT + g * (2 * GT) + j + 1)
                me(nc.vector.tensor_tensor(by_head(hn[:, j, :]), q_, qm[:, j, :].unsqueeze(2).to_broadcast([TP, AH, AD]), ALU.subtract))
                if j == GT - 1:
                    me.join(dve)
                    dve.nop().then_inc(s["q_ready"], 1)

            def q_scale(g, j):
                if j == 0:
                    dve.wait_ge(s["q_exp"], l * NG + g + 1)
                    settle(dve)
                h_ = by_head(hn[:, j, :])
                me.link(dve, nc.vector.tensor_reduce(qr[:, j, :], h_, AX.X, ALU.add))
                me.link(dve, nc.vector.reciprocal(qr[:, j, :], qr[:, j, :]))
                nc.vector.tensor_tensor(h_, h_, qr[:, j, :].unsqueeze(2).to_broadcast([TP, AH, AD]), ALU.mult).then_inc(s["hn_ready"], 1)

            def ffn_group(g, ahead):
                Tq, Yq, Fg = T + NT + g * (2 * GT), Y + (3 * NT + 2 * NG) + g * (2 * GT), F + g * (2 * FT)
                me.link(dve, nc.vector.tensor_tensor(zt(g * GT, GT), zt(g * GT, GT), bob[:, 0, :].unsqueeze(1).to_broadcast([TP, GT, D]), ALU.add))
                for j in range(GT):
                    lower(Tq + j, j)
                for j in range(GT):
                    add_y(Yq + j, j % 3, zt(g * GT + j), zt(g * GT + j))
                dve.wait_ge(s["y_used"], Yq + GT + 3)
                norm(Q + NG + g, Tq + GT, lambda j: zt(g * GT + j))
                for j in range(GT):
                    lower(Tq + GT + j, j)
                dve.wait_ge(s["hn_ready"], Tq + 2 * GT + 1)
                me(nc.vector.tensor_tensor(zt(g * GT, GT), zt(g * GT, GT), bob[:, 1, :].unsqueeze(1).to_broadcast([TP, GT, D]), ALU.add))
                me.join(dve)
                for u in range(2):
                    for f in range(FT):
                        lower_f(Fg + u * FT + f, f, SUB[u][1] * TS)
                        if f < GT and ahead:
                            (q_shift, q_scale)[u](g + 1, f)
                        if f == FT - 2:
                            messages(l * (2 * NG) + NG + g, (u,))
                    for i in range(SUB[u][1]):
                        t = SUB[u][0] + i
                        add_y(Yq + GT + t, i, zt(g * GT + t), zt(g * GT + t),
                              Fg + (u + 1) * FT - 1 if i == SUB[u][1] - 1 else None)
                me.join(dve)

            for j in range(GT):
                q_shift(0, j)
            for j in range(GT):
                q_scale(0, j)
            with loop(dve, NG - 1, (me, PER_G3)) as g:
                ffn_group(g, True)
            ffn_group(NG - 1, False)
            dve.wait_ge(s["y_used"], Y + Y_LAYER + 3)
            dve.wait_ge(s["gf_done"], F + F_LAYER + 2)
            dve.nop().then_inc(s["dve5"], 1)
            dve.nop().then_inc(s["par_used"], 1)
        stage_end(dve, 2)
        me.link(dve, nc.vector.memset(ex[:, :, :], 1.0))
        flat = score[:, :, :].rearrange("p c h -> p (c h)")
        me.link(dve, nc.vector.scalar_tensor_tensor(flat, flat, 0.2, flat, ALU.mult, ALU.max))
        nc.vector.tensor_reduce(hmax[:, :], score[:, :, :].rearrange("p c h -> p h c"), AX.X, ALU.max).then_inc(s["dve_go"], 1)
        dve.wait_ge(s["pe_go"], 4 + RR)
        me.link(dve, nc.vector.tensor_reduce(hm4[:, :], pb[0:MH, 0, 0:P], AX.X, ALU.max))
        nc.vector.tensor_scalar(hd4[:, :], ident[0:MH, 0:MH], hm4[:, 0:1], None, ALU.mult).then_inc(s["dve_go"], 1)
        dve.wait_ge(s["pe_go"], 5 + RR)
        me.link(dve, nc.vector.tensor_copy(hmb[:, :], pb[:, 1, 0:MH]))
        nc.vector.tensor_tensor(score[:, :, :], score[:, :, :],
                                hmb[:, :].unsqueeze(1).to_broadcast([P, NCH, MH]), ALU.subtract).then_inc(s["dve_go"], 1)
        stage_end(dve, 3)

        def weigh(n, b, load):
            dve.wait_ge(s[f"msg_ld{b}"], load)
            me(nc.vector.tensor_tensor(wm[:, b], msg[:, b].unsqueeze(2).to_broadcast([P, CG, MH, MF]),
                                       ex[:, bass.ds(n * CG, CG), 0:MH].unsqueeze(3).to_broadcast([P, CG, MH, MF]), ALU.mult))
            me(nc.vector.tensor_copy(ex_s[:, b], ex[:, bass.ds(n * CG, CG), :]))
            me.join(dve)
            dve.nop().then_inc(s["msg_used"], 1)

        me(nc.vector.memset(pa[:, :, :], 0.0))
        me(nc.vector.memset(pb[:, :, :], 0.0))
        me.join(dve)
        dve.nop().then_inc(s["msg_used"], 2)
        dve.nop().then_inc(s["win_used"], PR)
        dve.wait_ge(s["const"], 4)
        dve.wait_ge(s["act_go"], 1)

        def one_hots(n, b):
            nc.vector.tensor_tensor(oh[:, b], iota[:, 0:W].unsqueeze(1).to_broadcast([P, CG, W]),
                                    relT[:, bass.ds(n * CG, CG)].unsqueeze(2).to_broadcast([P, CG, W]),
                                    ALU.is_equal).then_inc(s["wm_ready"], 1)

        def add_windows(n):
            starts = [dve.value_load(base_i[0:1, bass.ds(n * PR + q, 1)], min_val=0, max_val=N - 1) for q in range(PR)]
            for q, at in enumerate(starts):
                dve.wait_ge(s["win_ps"], n * PR + (q + 1))
                dve.wait_ge(s["win_used"], n * PR + (q + PR))
                nc.vector.tensor_tensor(acc[:, :, bass.ds(at, W)], acc[:, :, bass.ds(at, W)],
                                        wbank[q][:, 0:3 * W].rearrange("p (k n) -> p k n", k=3), ALU.add).then_inc(s["win_used"], 1)

        weigh(0, 0, 16)
        one_hots(0, 0)
        with loop(dve, NCG // 2 - 1, (me, 4)) as i:
            weigh(i * 2 + 1, 1, i * 16 + 16)
            one_hots(i * 2 + 1, 1)
            add_windows(i * 2)
            weigh(i * 2 + 2, 0, i * 16 + 32)
            one_hots(i * 2 + 2, 0)
            add_windows(i * 2 + 1)
        weigh(NCG - 1, 1, 16 * (NCG // 2))
        one_hots(NCG - 1, 1)
        add_windows(NCG - 2)
        add_windows(NCG - 1)

        def rest_one_hots(k, column, nodes, one_hot, free, ready):
            dve.wait_ge(free, k + 1)
            settle(dve)
            nc.vector.tensor_tensor(one_hot[:, :], nodes[:, :], restT[:, bass.ds(column, 1)].to_broadcast([P, WS]),
                                    ALU.is_equal).then_inc(ready, 1)

        with dve.If(rest_flag(dve) == 1):
            mr = Tally(s["ra_w"])
            dve.nop().then_inc(s["ra_used"], 1)
            dve.nop().then_inc(s["ra_mm"], 1)
            with loop(dve, NCG, (mr, 3 + 4 * NW)) as n:
                dve.wait_ge(s["ra_ld"], n * 16 + 16)
                dve.wait_ge(s["ra_mm"], n * (NW * CG) + 1)
                settle(dve)
                mr(nc.vector.tensor_copy(iow[:, :], iota[:, :]))
                mr(nc.vector.tensor_tensor(wm[:, 0], msg[:, 0].unsqueeze(2).to_broadcast([P, CG, MH, MF]),
                                           ex[:, bass.ds(n * CG, CG), 0:MH].unsqueeze(3).to_broadcast([P, CG, MH, MF]), ALU.mult))
                mr(nc.vector.tensor_copy(ex_s[:, 0], ex[:, bass.ds(n * CG, CG), :]))
                mr.join(dve)
                dve.nop().then_inc(s["ra_used"], 1)
                with loop(dve, NW, (mr, 4)) as w:
                    for c in range(CG):
                        rest_one_hots((n * NW + w) * CG + c, n * CG + c, iow, ohs, s["ra_mm"], s["ra_oh"])
                    dve.wait_ge(s["ra_mm"], (n * NW + w) * CG + (CG + 1))
                    settle(dve)
                    for k, ps in enumerate((pb[:, 0, 0:WS], pb[:, 1, 0:WS], pg[:, 0, 0:WS])):
                        rows_ = MH + 1 if k == 2 else P
                        at = acc[0:rows_, k, bass.ds(w * WS, WS)]
                        mr(nc.vector.tensor_tensor(at, at, ps[0:rows_], ALU.add))
                    mr(nc.vector.tensor_scalar(iow[:, :], iow[:, :], float(WS), None, ALU.add))
                    mr.join(dve)
        stage_end(dve, 4)
        dve.wait_ge(s["xin_ld"], 16)
        me.link(dve, nc.vector.tensor_tensor(z[:, :, :], z[:, :, :], xin[:, :, :], ALU.add))
        for t in range(NT):
            dve.wait_ge(s["g_ps"], t + 1)
            ps = pa[0:TP, t % 2]
            me(nc.vector.tensor_scalar(den[:, 0, :], ps[:, 2 * P:2 * P + MH + 1], 1e-10, None, ALU.add))
            me(nc.vector.tensor_scalar(dinv[:, t:t + 1], ps[:, 2 * P + MH:2 * P + MH + 1], 1.0, None, ALU.max))
            me.join(dve)
            me.link(dve, nc.vector.reciprocal(den[:, 1, :], den[:, 0, :]))
            me.link(dve, nc.vector.tensor_tensor(gout[:, :].rearrange("p (h f) -> p h f", h=MH),
                                                 ps[:, 0:D].rearrange("p (h f) -> p h f", h=MH),
                                                 den[:, 1, 0:MH].unsqueeze(2).to_broadcast([TP, MH, MF]), ALU.mult))
            nc.vector.tensor_tensor(z[:, t, :], z[:, t, :], gout[:, :], ALU.add).then_inc(s["g_used"], 1)
        me.link(dve, nc.vector.reciprocal(dinv[:, :], dinv[:, :]))
        stage_end(dve, 5)

        def gate_logits(q0, t0, y0):
            with loop(dve, NG, (me, 2 * GT + 1)) as g:
                norm(g + q0, g * GT + t0, lambda j: zt(g * GT + j))
                for j in range(GT):
                    lower(g * GT + (t0 + j), j)
                for j in range(GT):
                    dve.wait_ge(s["y_ps"], g * GT + (y0 + j + 1))
                    nc.vector.tensor_tensor(lg[:, bass.ds(g * GT + j, 1), :].rearrange("p o e -> p (o e)"),
                                            pa[0:TP, j % 3, 0:NE], lgb[:, :], ALU.add).then_inc(s["y_used"], 1)
            dve.wait_ge(s["y_used"], y0 + NT + 3)

        def gate_softmax(n):
            wide = [TP, NT, NE]
            me.link(dve, nc.vector.tensor_reduce(lgm[:, :], lg[:, :, :], AX.X, ALU.max))
            nc.vector.tensor_tensor(lg[:, :, :], lg[:, :, :], lgm[:, :].unsqueeze(2).to_broadcast(wide), ALU.subtract).then_inc(s["ex_go"], 1)
            dve.wait_ge(s["ex_go"], n + 2)
            me.link(dve, nc.vector.tensor_reduce(lgm[:, :], lg[:, :, :], AX.X, ALU.add))
            me.link(dve, nc.vector.reciprocal(lgm[:, :], lgm[:, :]))
            me.link(dve, nc.vector.tensor_tensor(lg[:, :, :], lg[:, :, :], lgm[:, :].unsqueeze(2).to_broadcast(wide), ALU.mult))

        def bias_sums(y0, cw0, lg0):
            with dve.Fori(0, NG) as g:
                nc.vector.tensor_copy(cws[:, :, :], lg[:, bass.ds(g * GT, GT), :]).then_inc(s["cw_go"], 1)
                dve.wait_ge(s["lg_go"], g + (lg0 + 1))
                dve.wait_ge(s["cw_go"], g * 2 + (cw0 + 1))
                settle(dve)
                nc.vector.tensor_copy(hn[0:NE, 0:4, 0:TP],
                                      pb[0:NE, 0, :].rearrange("p (j c) -> p j c", j=4)[:, :, 0:TP]).then_inc(s["cwt"], 1)
                nc.vector.tensor_copy(hn[0:NE, 4, 0:TP], pb[0:NE, 1, 0:TP]).then_inc(s["cwt"], 1)
                dve.wait_ge(s["cwt"], g * 2 + (cw0 + 2))
                dve.nop().then_inc(s["cw_go"], 1)
                for j in range(GT):
                    add_y(g * GT + (y0 + j), j % 3, zt(g * GT + j), zt(g * GT + j))

        def weights_of(e, g, y):
            dve.wait_ge(s["y_used"], y + 3)
            settle(dve)
            tiles = slice(g * GT, (g + 1) * GT) if isinstance(g, int) else bass.ds(g * GT, GT)
            expert = slice(e, e + 1) if isinstance(e, int) else bass.ds(e, 1)
            nc.vector.tensor_copy(cwg[:, 0, :], lg[:, tiles, expert].rearrange("p t o -> p (t o)")).then_inc(s["cwg_in"], 1)

        def add_weighted(y, bank, j, t, done=None):
            if done is None:
                dve.wait_ge(s["y_ps"], y + 1)
            else:
                dve.wait_ge(s["act_used"], done)
                dve.nop().then_inc(s["y_ps"], 1)
            nc.vector.scalar_tensor_tensor(zt(t), bank[0:TP, 0:D], cwg[:, 0, j:j + 1], zt(t),
                                           ALU.mult, ALU.add).then_inc(s["y_used"], 1)

        dve.wait_ge(s["const"], 5)
        dve.wait_ge(s["p6_ld"], 48)
        split([w[:, :, :] for w in gw], gwf[:, :, :])
        me.join(dve)
        dve.nop().then_inc(s["dve5"], 1)

        gate_logits(Q_MOE, T_MOE, Y_MOE)
        gate_softmax(0)
        wide = [TP, NT, NE, NE]
        p_j = lg[:, :, :].unsqueeze(2).to_broadcast(wide)
        p_e = lg[:, :, :].unsqueeze(3).to_broadcast(wide)
        me(nc.vector.tensor_tensor(cmp[:, 0], p_j, p_e, ALU.is_gt))
        me.link(dve, nc.vector.tensor_tensor(cmp[:, 1], p_j, p_e, ALU.is_equal))
        me.link(dve, nc.vector.tensor_tensor(cmp[:, 1], cmp[:, 1], tri[:, :, :].unsqueeze(1).to_broadcast(wide), ALU.mult))
        me.link(dve, nc.vector.tensor_tensor(cmp[:, 0], cmp[:, 0], cmp[:, 1], ALU.add))
        me.link(dve, nc.vector.tensor_reduce(rank[:, :, :], cmp[:, 0], AX.X, ALU.add))
        me.link(dve, nc.vector.tensor_scalar(rank[:, :, :], rank[:, :, :], 1.5, None, ALU.is_lt))
        me.link(dve, nc.vector.tensor_tensor(lg[:, :, :], lg[:, :, :], rank[:, :, :], ALU.mult))
        bias_sums(Y_BIAS, 0, 0)
        def moe_group(e, g, ahead):
            Fg, y = (e * NG + g) * (2 * MT) + F_MOE, (e * NG + g) * GT + Y_EXP
            for u in range(2):
                for f in range(1, MT):
                    lower_f(Fg + (u * MT + f), f, SUB[u][1] * TS)
                if u == 0 or ahead:
                    lower_f(Fg + (u + 1) * MT, 0, SUB[1 - u][1] * TS)
                if u == 0:
                    weights_of(e, g, y)
                    dve.wait_ge(s["cwg_in"], e * NG + g + 1)
                for i in range(SUB[u][1]):
                    t = SUB[u][0] + i
                    add_weighted(y + t, unit_banks[u][i], t, g * GT + t,
                                 Fg + ((u + 1) * MT + 4) if i == SUB[u][1] - 1 else None)

        lower_f(F_MOE, 0, SUB[0][1] * TS)
        with dve.Fori(0, NE - 1) as e:
            with dve.Fori(0, NG) as g:
                moe_group(e, g, True)
        with dve.Fori(0, NG - 1) as g:
            moe_group(NE - 1, g, True)
        moe_group(NE - 1, NG - 1, False)
        dve.wait_ge(s["y_used"], Y_L1 + 3)
        stage_end(dve, 6)

        with loop(dve, NG, (me, 3 * GT + 1)) as g:
            norm_stats(T_L1, lambda j: zt(g * GT + j))
            dve.wait_ge(s["sdr"], g + (Q_ROWS + 1))
            me.link(dve, nc.vector.reciprocal(rstd[:, :], sd[:, :]))
            dve.wait_ge(s["t1_st"], g * 16 + 16)
            settle(dve)
            for j in range(GT):
                me(nc.vector.tensor_scalar(kv[:, j, 0, :], zt(g * GT + j), mv[:, j, 0:1], rstd[:, j:j + 1], ALU.subtract, ALU.mult))
            me.join(dve)
            dve.nop().then_inc(s["rows_ready"], 1)
        for b in range(2):
            nc.vector.tensor_copy(idx1[:, b].rearrange("p u c -> p (u c)"),
                                  srcT[:, b * UB * UC:(b + 1) * UB * UC]).then_inc(s["ix1"], 1)
        dve.nop().then_inc(s["rw_used"], UB)
        dve.wait_ge(s["const"], 6)

        def one_hots1(n, b):
            nc.vector.tensor_tensor(oh1[:, b], iota[:, 0:W].unsqueeze(1).to_broadcast([P, UC, W]),
                                    (relT[:, n * UC:(n + 1) * UC] if isinstance(n, int) else relT[:, bass.ds(n * UC, UC)]).unsqueeze(2).to_broadcast([P, UC, W]),
                                    ALU.is_equal).then_inc(s["o1_ready"], 1)

        def add_unit_windows(slot, units, banks):
            for k in units:
                n, b = slot * SU + k, k % UB
                one_hots1(n + 1, (k + 1) % UB)
                at = dve.value_load(base_i[0:1, bass.ds(n, 1)], min_val=0, max_val=N - 1)
                dve.wait_ge(s["win_ps"], slot * SU + (NPR + 1 + k))
                dve.wait_ge(s["win_used"], slot * SU + (NPR + PR + k))
                nc.vector.tensor_tensor(acc1[:, :, bass.ds(at, W)], acc1[:, :, bass.ds(at, W)],
                                        banks[k % 2][:, 0:H * W].rearrange("p (k n) -> p k n", k=H), ALU.add).then_inc(s["win_used"], 1)
                dve.nop().then_inc(s["rw_used"], 1)
                if b == UB - 1:
                    dve.wait_ge(s[f"rw{b}"], slot * (SB * 16 * UC) + (k // UB + 1) * (16 * UC))
                    settle(dve)
                    nc.vector.tensor_copy(idx1[:, k // UB % 2].rearrange("p u c -> p (u c)"),
                                          srcT[:, bass.ds((n + 1 + UB) * UC, UB * UC)]).then_inc(s["ix1"], 1)

        one_hots1(0, 0)
        dve.wait_ge(s["p7_ld"], 336)
        for h in range(H):
            w3 = qw[:, h, :].rearrange("p (a x) -> p a x", x=3 * AD)
            for k in range(2):
                split([w[:, h, k, :].rearrange("p (a c) -> p a c", c=AD) for w in kvw], w3[:, :, (k + 1) * AD:(k + 2) * AD])
            split([w[:, h, :] for w in awo], awr[:, h, :])
            me(nc.vector.tensor_copy(rwf[:, h, :].rearrange("p (a c) -> p a c", c=AD), w3[:, :, 0:AD]))
        me(nc.vector.tensor_tensor(bsum[:, 2, :], bsum[:, 0, :], bsum[:, 1, :], ALU.add))
        me(nc.vector.memset(kva[:, :, :], 0.0))
        me(nc.vector.memset(pb[:, 0, 0:D], 0.0))
        me.join(dve)
        dve.nop().then_inc(s["dve7"], 1)

        def add_kv(g):
            dve.wait_ge(s["g7"], g + 1)
            settle(dve)
            me.join(dve)
            me.link(dve, nc.vector.tensor_tensor(kva[:, :, :], kva[:, :, :], pb[:, 0, 0:D].rearrange("p (h c) -> p h c", h=H), ALU.add))

        kv_all = kv[:, :, :, :].rearrange("p t k (a c) -> p (t k a) c", c=AD)
        kvq_all = kvq[:, :, :, :].rearrange("p t k (a c) -> p (t k a) c", c=AD)
        kvm_all = kvm[:, :, :].rearrange("p t a -> p (t a)")
        kvm_wide = kvm_all.unsqueeze(2).to_broadcast([TP, GT * 2 * AH, AD])

        def kv_group(g):
            add_unit_windows(g, range(0, 2), kv_banks)
            norm_stats(g * GT + T_L1, lambda j: zt(g * GT + j))
            add_unit_windows(g, range(2, 4), kv_banks)
            norm_apply(g + Q_L1, g * GT + T_L1, lambda j: zt(g * GT + j))
            dve.wait_ge(s["hn_ready"], g * GT + (T_L1 + GT) + 1)
            settle(dve)
            me.link(dve, nc.vector.tensor_tensor(zt(g * GT, GT), zt(g * GT, GT), hn[:, :, :], ALU.add))
            me(nc.vector.tensor_tensor(zt(g * GT, GT), zt(g * GT, GT), bsum[:, 2, :].unsqueeze(1).to_broadcast([TP, GT, D]), ALU.add))
            for j in range(GT):
                lower(g * GT + (T_L1 + j), j)
            add_unit_windows(g, range(4, 6), kv_banks)
            for j in range(GT):
                y = g * (2 * GT) + (2 * j + Y_L1)
                for k in range(2):
                    dve.wait_ge(s["y_ps"], y + k + 1)
                    nc.vector.tensor_tensor(kv[:, j, k, :].rearrange("p (a c) -> p a c", c=AD),
                                            pa[0:TP, (2 * j + k) % 3, 0:D].rearrange("p (a c) -> p a c", c=AD),
                                            bkv[:, :].rearrange("p (a x) -> p a x", x=3 * AD)[:, :, (k + 1) * AD:(k + 2) * AD],
                                            ALU.add).then_inc(s["y_used"], 1)
                if j % 2:
                    add_unit_windows(g, (6 + j // 2,), kv_banks)
            dve.wait_ge(s["y_used"], g * (2 * GT) + (Y_L1 + 2 * GT + 3))
            settle(dve)
            me.link(dve, nc.vector.tensor_reduce(kvm_all, kv_all, AX.X, ALU.add))
            me.link(dve, nc.vector.tensor_scalar(kvm_all, kvm_all, 1.0 / AD, None, ALU.mult))
            nc.vector.tensor_tensor(kv_all, kv_all, kvm_wide, ALU.subtract).then_inc(s["kv_go"], 1)
            add_unit_windows(g, range(8, 11), kv_banks)
            dve.wait_ge(s["sq_go"], g * 2 + 1)
            settle(dve)
            me.link(dve, nc.vector.tensor_reduce(kvm_all, kvq_all, AX.X, ALU.add))
            nc.vector.tensor_scalar(kvm_all, kvm_all, 1.0 / AD, EPS, ALU.mult, ALU.add).then_inc(s["kv_go"], 1)
            add_unit_windows(g, range(11, 14), kv_banks)
            dve.wait_ge(s["sq_go"], g * 2 + 2)
            me.link(dve, nc.vector.reciprocal(kvm_all, kvm_all))
            me.link(dve, nc.vector.tensor_tensor(kv_all, kv_all, kvm_wide, ALU.mult))
            for n, op in enumerate((ALU.mult, ALU.add)):
                add_unit_windows(g, range(14 + 3 * n, 17 + 3 * n), kv_banks)
                for k in range(2):
                    part = kv[:, :, k, :].rearrange("p t (a c) -> p t a c", c=AD)
                    me(nc.vector.tensor_tensor(part, part, lnkv[:, k, n, :].unsqueeze(1).unsqueeze(1).to_broadcast([TP, GT, AH, AD]), op))
                me.join(dve)

        with loop(dve, NG, (me, 2 * GT + 1 + 2 + 2 + 1 + 2 + 4 + 1)) as g:
            kv_group(g)
            add_kv(g)
            dve.nop().then_inc(s["kv_ready"], 1)
        add_kv(NG)
        for h in range(H):
            me.link(dve, nc.vector.scalar_tensor_tensor(kva[:, h, :], kva[:, h, :], 1.0 / N, blocks[:, :], ALU.mult, ALU.mult))
        dve.wait_ge(s["win_used"], NG * SU + NPR + PR)
        dve.wait_ge(s["pe7"], 1)
        nc.vector.tensor_copy(qT[:, :, :], pt[:, :, 0:D]).then_inc(s["dve7"], 1)
        dve.nop().then_inc(s["dve7"], 1)
        dve.wait_ge(s["pe7"], 2)
        me(nc.vector.tensor_copy(rwf[:, :, :], pa[:, 0:H, 0:D]))
        me(nc.vector.tensor_copy(rb[:, :], pa[:, 2, 0:H]))
        me.join(dve)
        for h in range(H):
            me(nc.vector.tensor_tensor(rwf[:, h, h * P:(h + 1) * P], rwf[:, h, h * P:(h + 1) * P], ident[:, :], ALU.add))
        me.join(dve)
        split([w[:, :, :] for w in rw], rwf[:, :, :])
        split([w[:, :, :] for w in mw], mraw[:, :, :])
        me.join(dve)
        dve.nop().then_inc(s["dve7"], 1)
        with dve.Fori(0, NG) as g:
            for u in range(2):
                F = (g * 2 + u) * 4 + F_RET
                for f in range(4):
                    lower_f(F + f, f, SUB[u][1] * TS)
                    if f % 2:
                        add_unit_windows(g + NG, range(u * 10 + 2 * (f - 1), u * 10 + 2 * (f + 1)), ret_banks)
                for i in range(SUB[u][1]):
                    t = SUB[u][0] + i
                    add_y(g * GT + (Y_RET + t), i, zt(g * GT + t), zt(g * GT + t), F + 3 if i == SUB[u][1] - 1 else None)
                add_unit_windows(g + NG, range(u * 10 + 8, u * 10 + 10), ret_banks)
        dve.wait_ge(s["y_used"], Y_AGG + 3)
        stage_end(dve, 7)
        with dve.If(rest_flag(dve) == 1):
            mr = Tally(s["rb_w"])
            dve.nop().then_inc(s["rb_mm"], 1)
            with loop(dve, NU, (mr, 1 + 3 * NW)) as n:
                dve.wait_ge(s["rb_mm"], n * (NW * UC) + 1)
                settle(dve)
                nc.vector.tensor_copy(idx1[:, 0, 0, :], srcT[:, bass.ds(n * UC, UC)]).then_inc(s["rb_in"], 1)
                mr(nc.vector.tensor_copy(iow1[:, :], iota[:, :]))
                mr.join(dve)
                dve.wait_ge(s["rb_ld"], n * (16 * UC) + 16 * UC)
                settle(dve)
                with loop(dve, NW, (mr, 3)) as w:
                    for c in range(UC):
                        rest_one_hots((n * NW + w) * UC + c, n * UC + c, iow1, ohs1, s["rb_mm"], s["rb_oh"])
                    dve.wait_ge(s["rb_mm"], (n * NW + w) * UC + (UC + 1))
                    settle(dve)
                    for k in range(H):
                        at_ = acc1[:, k, bass.ds(w * WS, WS)]
                        mr(nc.vector.tensor_tensor(at_, at_, pb[:, k, 0:WS], ALU.add))
                    mr(nc.vector.tensor_scalar(iow1[:, :], iow1[:, :], float(WS), None, ALU.add))
                    mr.join(dve)
            dve.nop().then_inc(s["rb_sum"], 1)
        for t in range(NT):
            dve.wait_ge(s["y_ps"], Y_AGG + t + 1)
            me.link(dve, nc.vector.tensor_copy(g1[:, t, :], pb[0:TP, t % 2, 0:D]))
            nc.vector.scalar_tensor_tensor(g1[:, t, :], pa[0:TP, t % 3, 0:D], dinv[:, t:t + 1], g1[:, t, :],
                                           ALU.mult, ALU.add).then_inc(s["y_used"], 1)
        dve.wait_ge(s["act9"], NT + 1)
        me.link(dve, nc.vector.reciprocal(ss[:, :], ss[:, :]))
        for t in range(NT):
            me(nc.vector.scalar_tensor_tensor(z[:, t, :], g1[:, t, :], ss[:, t:t + 1], z[:, t, :], ALU.mult, ALU.add))
        me.join(dve)
        stage_end(dve, 8)
        dve.wait_ge(s["p9_ld"], 16 * 13)
        split([w[:, :, :] for w in gw], gwf[:, :, :])
        me.join(dve)
        dve.nop().then_inc(s["dve7"], 1)
        nc.vector.tensor_scalar(bnp[:, :, 3, :], bnp[:, :, 3, :], 1e-3, None, ALU.add).then_inc(s["bn_go"], 1)
        dve.wait_ge(s["bn_go"], 2)
        me.link(dve, nc.vector.reciprocal(bnp[:, :, 3, :], bnp[:, :, 3, :]))
        me(nc.vector.tensor_tensor(bnp[:, :, 0, :], bnp[:, :, 0, :], bnp[:, :, 3, :], ALU.mult))
        me.link(dve, nc.vector.tensor_tensor(bnp[:, :, 4, :], bnp[:, :, 4, :], bnp[:, :, 2, :], ALU.subtract))
        me.link(dve, nc.vector.tensor_tensor(bnp[:, :, 4, :], bnp[:, :, 4, :], bnp[:, :, 0, :], ALU.mult))
        for n in range(2):
            by_e = [bnp[:, n, k, :].rearrange("p (e h) -> p e h", h=H) for k in (0, 1, 4)]
            me(nc.vector.tensor_copy(bns[:, :, 2 * n, :], by_e[0]))
            me(nc.vector.tensor_tensor(bns[:, :, 2 * n + 1, :], by_e[2], by_e[1], ALU.add))
        me.join(dve)
        dve.nop().then_inc(s["bn_go"], 1)
        gate_logits(Q_FFN1, T_FFN1, Y_GATE1)
        gate_softmax(2)
        bias_sums(Y_BIAS1, 2 * NG, NG)

        def lower9(F, slot, u):
            n = SUB[u][1] * TS
            for f in range(2):
                dve.wait_ge(s["f_hi"], F + (3 + f))
                nc.vector.tensor_tensor(act9[1][:, slot + f, 0:n], gf[:, f, 0:n], act9[0][:, slot + f, 0:n],
                                        ALU.subtract).then_inc(s["f_lo"], 1)

        def add_unit(u, n, y, t):
            tiles = SUB[u][1]
            for i in range(tiles):
                add_weighted(y + i, unit_banks[u][i], SUB[u][0] + i, t + i, n * 4 + (F_FFN1 + 8) if i == tiles - 1 else None)

        def ffn_expert(e, first, last):
            def two(g, head, tail):
                n, y = (e * NG + g) * 2, (e * NG + g) * GT + Y_EXP1
                lower9(n * 4 + (F_FFN1 + 2), 2, 1)
                if not (head and first):
                    add_unit(1, n - 1, y - SUB[1][1], NT - SUB[1][1] if head else g * GT - SUB[1][1])
                lower9(n * 4 + (F_FFN1 + 4), 4, 0)
                end = tail and last
                if not end:
                    lower9(n * 4 + (F_FFN1 + 6), 0, 0)
                weights_of(e, g, y)
                dve.wait_ge(s["cwg_in"], e * NG + g + (NE * NG + 1))
                add_unit(0, n, y, g * GT)
                lower9(n * 4 + (F_FFN1 + (6 if end else 8)), 4, 1)
            two(0, True, False)
            with dve.Fori(1, NG - 1) as g:
                two(g, False, False)
            two(NG - 1, False, True)

        lower9(F_FFN1, 0, 0)
        ffn_expert(0, True, False)
        with dve.Fori(0, NE // 2 - 1) as ep:
            ffn_expert(ep * 2 + 1, False, False)
            ffn_expert(ep * 2 + 2, False, False)
        ffn_expert(NE - 1, False, True)
        add_unit(1, NE * NG * 2 - 1, Y_EXP1 + NE * NT - SUB[1][1], NT - SUB[1][1])
        stage_end(dve, 9)


def kernel(**inputs):
    import numpy as _np
    import concourse.bacc as _bacc
    from concourse import mybir as _mybir
    from concourse.bass_utils import run_bass_kernel_spmd as _run

    nc = _bacc.Bacc("TRN2", target_bir_lowering=False, num_devices=1)
    arrays, args = {}, {}
    for name, value in inputs.items():
        v = _np.ascontiguousarray(value)
        arrays[f"in_{name}_dram"] = v
        args[name] = nc.dram_tensor(f"in_{name}_dram", v.shape, _mybir.dt.from_np(v.dtype), kind="ExternalInput").ap()
    out = nc.dram_tensor("out_0_dram", (N, D), _mybir.dt.float32, kind="ExternalOutput").ap()
    gps_kernel(nc, args, out)
    r = _run(nc, [arrays], core_ids=[0])
    return r.results[0]["out_0_dram"]
```
